# Optimizing a Trainium2 kernel written in Bass

```python
import numpy as np
import jax
import jax.numpy as jnp

def _softmax(x, axis=-1):
    return jax.nn.softmax(x, axis=axis)

def _gelu(x):
    return jax.nn.gelu(x, approximate=True)

def _silu(x):
    return jax.nn.silu(x)

def _sigmoid(x):
    return jax.nn.sigmoid(x)

def _layernorm(x, axis=-1, eps=1e-05):
    m = jnp.mean(x, axis=axis, keepdims=True)
    v = jnp.var(x, axis=axis, keepdims=True)
    return (x - m) / jnp.sqrt(v + eps)

def _scatter_add(tgt, idx, src, axis=0):
    return tgt.at[idx].add(src)

def _segment_sum(src, seg, n):
    return jax.ops.segment_sum(src, seg, n)
kernel_name = 'mk_recurrent_d1_jaxref_r8_784f33'

def setup_inputs(seed: int=0):
    np.random.seed(seed)
    _w = jnp.asarray

    def _L0_attn_setup():
        import jax, jax.numpy as jnp
        import numpy as np
        import math
        EPS_LN = 1e-05
        SCALE = 16.0

        def layer_norm(x, g):
            mean = jnp.mean(x, axis=-1, keepdims=True)
            var = jnp.var(x, axis=-1, keepdims=True)
            return (x - mean) * jax.lax.rsqrt(var + EPS_LN) * g

        def l2norm(t):
            n = jnp.linalg.norm(t, axis=-1, keepdims=True)
            return t / jnp.maximum(n, 1e-12)
        key = jax.random.key(seed)
        ks = jax.random.split(key, 4)
        b, n, dim, h, dh = (4, 256, 128, 8, 64)
        inner = h * dh
        x = jax.random.normal(ks[0], (b, n, dim), dtype=jnp.float32)
        Wq = jax.random.normal(ks[1], (dim, inner), dtype=jnp.float32) * dim ** (-0.5)
        Wkv = jax.random.normal(ks[2], (dim, 2 * dh), dtype=jnp.float32) * dim ** (-0.5)
        Wout = jax.random.normal(ks[3], (inner, dim), dtype=jnp.float32) * inner ** (-0.5)
        norm_g = jnp.ones((dim,), dtype=jnp.float32)
        out_norm_g = jnp.ones((dim,), dtype=jnp.float32)
        return {'x': x, 'norm_g': norm_g, 'Wq': Wq, 'Wkv': Wkv, 'Wout': Wout, 'out_norm_g': out_norm_g}
    _L0_attn_in = _L0_attn_setup()

    def _L0_ffn_setup():
        import jax, jax.numpy as jnp
        import numpy as np
        DIM = 128
        DEPTH = 2
        HEADS = 8
        DIM_HEAD = 64
        WINDOW = 64
        INNER = HEADS * DIM_HEAD
        HID = int(DIM * 4 * 2 / 3)
        B, N = (2, 1024)
        QK_SCALE = 8.0

        def shift_token(t):
            t1, t2 = jnp.split(t, 2, axis=-1)
            t2 = jnp.pad(t2, ((0, 0), (1, 0), (0, 0)))[:, :-1]
            return jnp.concatenate([t1, t2], axis=-1)

        def l2norm(t):
            return t / jnp.clip(jnp.linalg.norm(t, axis=-1, keepdims=True), 1e-12)

        def rotate_half(x):
            x1, x2 = jnp.split(x, 2, axis=-1)
            return jnp.concatenate([-x2, x1], axis=-1)

        def rotary_xpos(q, k):
            n = q.shape[-2]
            half_idx = jnp.arange(0, DIM_HEAD, 2, dtype=jnp.float32)
            inv_freq = 1.0 / 10000.0 ** (half_idx / DIM_HEAD)
            t = jnp.arange(n, dtype=jnp.float32)
            freqs = t[:, None] * inv_freq[None, :]
            freqs = jnp.concatenate([freqs, freqs], axis=-1)
            base = (half_idx + 0.4 * DIM_HEAD) / (1.4 * DIM_HEAD)
            power = (t - n // 2) / float(WINDOW // 2)
            scale = base[None, :] ** power[:, None]
            scale = jnp.concatenate([scale, scale], axis=-1)
            cos, sin = (jnp.cos(freqs), jnp.sin(freqs))
            q = q * cos * scale + rotate_half(q) * sin * scale
            k = k * cos / scale + rotate_half(k) * sin / scale
            return (q, k)

        def local_attention(q, k, v):
            b, h, n, d = q.shape
            w = n // WINDOW
            bq = q.reshape(b, h, w, WINDOW, d) * QK_SCALE
            bk = k.reshape(b, h, w, WINDOW, d)
            bv = v.reshape(b, h, w, WINDOW, d)

            def look_around(t):
                p = jnp.pad(t, ((0, 0), (0, 0), (1, 0), (0, 0), (0, 0)))
                return jnp.concatenate([p[:, :, :w], p[:, :, 1:]], axis=3)
            bk, bv = (look_around(bk), look_around(bv))
            bt = jnp.arange(n).reshape(w, WINDOW)
            btp = jnp.pad(bt, ((1, 0), (0, 0)), constant_values=-1)
            btk = jnp.concatenate([btp[:w], btp[1:]], axis=1)
            sim = jnp.einsum('bhwid,bhwjd->bhwij', bq, bk)
            i = bt[:, :, None]
            j = btk[:, None, :]
            mask = (i < j) | (i > j + WINDOW) | (j == -1)
            sim = jnp.where(mask, -jnp.finfo(sim.dtype).max, sim)
            attn = jax.nn.softmax(sim, axis=-1)
            out = jnp.einsum('bhwij,bhwjd->bhwid', attn, bv)
            return out.reshape(b, h, n, d)

        def _layer(x, wqkv, qs, ksc, wo, lg, lb, w1, b1, w2, b2):
            b, n, _ = x.shape
            h = shift_token(x)
            qkv = h @ wqkv
            q, k, v = jnp.split(qkv, 3, axis=-1)
            to_heads = lambda t: t.reshape(b, n, HEADS, DIM_HEAD).transpose(0, 2, 1, 3)
            q, k, v = (to_heads(q), to_heads(k), to_heads(v))
            q = l2norm(q) * qs
            k = l2norm(k) * ksc
            q, k = rotary_xpos(q, k)
            o = local_attention(q, k, v)
            o = o.transpose(0, 2, 1, 3).reshape(b, n, INNER)
            x = x + o @ wo
            h = shift_token(x)
            mu = h.mean(-1, keepdims=True)
            var = h.var(-1, keepdims=True)
            h = (h - mu) / jnp.sqrt(var + 1e-05) * lg + lb
            h = h @ w1 + b1
            a, g = jnp.split(h, 2, axis=-1)
            h = a * jax.nn.gelu(g, approximate=False)
            x = x + h @ w2 + b2
            return x
        key = jax.random.key(seed)
        ks = jax.random.split(key, 6)
        return {'x': jax.random.normal(ks[0], (B, N, DIM), jnp.float32), 'wqkv': jax.random.normal(ks[1], (DEPTH, DIM, 3 * INNER), jnp.float32) * 0.02, 'q_scale': jnp.ones((DEPTH, DIM_HEAD), jnp.float32), 'k_scale': jnp.ones((DEPTH, DIM_HEAD), jnp.float32), 'wo': jax.random.normal(ks[2], (DEPTH, INNER, DIM), jnp.float32) * 0.02, 'ln_g': jnp.ones((DEPTH, DIM), jnp.float32), 'ln_b': jnp.zeros((DEPTH, DIM), jnp.float32), 'w1': jax.random.normal(ks[3], (DEPTH, DIM, 2 * HID), jnp.float32) * 0.02, 'b1': jnp.zeros((DEPTH, 2 * HID), jnp.float32), 'w2': jax.random.normal(ks[4], (DEPTH, HID, DIM), jnp.float32) * 0.02, 'b2': jnp.zeros((DEPTH, DIM), jnp.float32)}
    _L0_ffn_in = _L0_ffn_setup()
    _d = {'L0_attn_x': _L0_attn_in['x'], 'L0_attn_norm_g': _L0_attn_in['norm_g'], 'L0_attn_Wq': _L0_attn_in['Wq'], 'L0_attn_Wkv': _L0_attn_in['Wkv'], 'L0_attn_Wout': _L0_attn_in['Wout'], 'L0_attn_out_norm_g': _L0_attn_in['out_norm_g'], 'L0_ffn_wqkv': _L0_ffn_in['wqkv'], 'L0_ffn_q_scale': _L0_ffn_in['q_scale'], 'L0_ffn_k_scale': _L0_ffn_in['k_scale'], 'L0_ffn_wo': _L0_ffn_in['wo'], 'L0_ffn_ln_g': _L0_ffn_in['ln_g'], 'L0_ffn_ln_b': _L0_ffn_in['ln_b'], 'L0_ffn_w1': _L0_ffn_in['w1'], 'L0_ffn_b1': _L0_ffn_in['b1'], 'L0_ffn_w2': _L0_ffn_in['w2'], 'L0_ffn_b2': _L0_ffn_in['b2']}
    _x0 = _d['L0_attn_x']
    _d['L0_attn_x'] = jax.random.normal(jax.random.fold_in(jax.random.key(seed), 1), (2, 1024, 128), dtype=_x0.dtype)
    del _x0
    return _d

def reference(L0_attn_x, L0_attn_norm_g, L0_attn_Wq, L0_attn_Wkv, L0_attn_Wout, L0_attn_out_norm_g, L0_ffn_wqkv, L0_ffn_q_scale, L0_ffn_k_scale, L0_ffn_wo, L0_ffn_ln_g, L0_ffn_ln_b, L0_ffn_w1, L0_ffn_b1, L0_ffn_w2, L0_ffn_b2):

    def _L0_attn_ref(x, norm_g, Wq, Wkv, Wout, out_norm_g):
        import jax, jax.numpy as jnp
        import numpy as np
        import math
        EPS_LN = 1e-05
        SCALE = 16.0

        def layer_norm(x, g):
            mean = jnp.mean(x, axis=-1, keepdims=True)
            var = jnp.var(x, axis=-1, keepdims=True)
            return (x - mean) * jax.lax.rsqrt(var + EPS_LN) * g

        def l2norm(t):
            n = jnp.linalg.norm(t, axis=-1, keepdims=True)
            return t / jnp.maximum(n, 1e-12)
        b, n, dim = x.shape
        h = 8
        dh = Wkv.shape[-1] // 2
        xn = layer_norm(x, norm_g)
        q = xn @ Wq
        kv = xn @ Wkv
        k, v = (kv[..., :dh], kv[..., dh:])
        q = q.reshape(b, n, h, dh).transpose(0, 2, 1, 3)
        q = q * SCALE
        q = l2norm(q)
        k = l2norm(k)
        rs = math.sqrt(SCALE)
        q = q * rs
        k = k * rs
        sim = jnp.einsum('bhid,bjd->bhij', q, k)
        attn = jax.nn.softmax(sim.astype(jnp.float32), axis=-1).astype(sim.dtype)
        out = jnp.einsum('bhij,bjd->bhid', attn, v)
        out = out.transpose(0, 2, 1, 3).reshape(b, n, h * dh)
        out = out @ Wout
        return layer_norm(out, out_norm_g)

    def _L0_ffn_ref(x, wqkv, q_scale, k_scale, wo, ln_g, ln_b, w1, b1, w2, b2):
        import jax, jax.numpy as jnp
        import numpy as np
        DIM = 128
        DEPTH = 2
        HEADS = 8
        DIM_HEAD = 64
        WINDOW = 64
        INNER = HEADS * DIM_HEAD
        HID = int(DIM * 4 * 2 / 3)
        B, N = (2, 1024)
        QK_SCALE = 8.0

        def shift_token(t):
            t1, t2 = jnp.split(t, 2, axis=-1)
            t2 = jnp.pad(t2, ((0, 0), (1, 0), (0, 0)))[:, :-1]
            return jnp.concatenate([t1, t2], axis=-1)

        def l2norm(t):
            return t / jnp.clip(jnp.linalg.norm(t, axis=-1, keepdims=True), 1e-12)

        def rotate_half(x):
            x1, x2 = jnp.split(x, 2, axis=-1)
            return jnp.concatenate([-x2, x1], axis=-1)

        def rotary_xpos(q, k):
            n = q.shape[-2]
            half_idx = jnp.arange(0, DIM_HEAD, 2, dtype=jnp.float32)
            inv_freq = 1.0 / 10000.0 ** (half_idx / DIM_HEAD)
            t = jnp.arange(n, dtype=jnp.float32)
            freqs = t[:, None] * inv_freq[None, :]
            freqs = jnp.concatenate([freqs, freqs], axis=-1)
            base = (half_idx + 0.4 * DIM_HEAD) / (1.4 * DIM_HEAD)
            power = (t - n // 2) / float(WINDOW // 2)
            scale = base[None, :] ** power[:, None]
            scale = jnp.concatenate([scale, scale], axis=-1)
            cos, sin = (jnp.cos(freqs), jnp.sin(freqs))
            q = q * cos * scale + rotate_half(q) * sin * scale
            k = k * cos / scale + rotate_half(k) * sin / scale
            return (q, k)

        def local_attention(q, k, v):
            b, h, n, d = q.shape
            w = n // WINDOW
            bq = q.reshape(b, h, w, WINDOW, d) * QK_SCALE
            bk = k.reshape(b, h, w, WINDOW, d)
            bv = v.reshape(b, h, w, WINDOW, d)

            def look_around(t):
                p = jnp.pad(t, ((0, 0), (0, 0), (1, 0), (0, 0), (0, 0)))
                return jnp.concatenate([p[:, :, :w], p[:, :, 1:]], axis=3)
            bk, bv = (look_around(bk), look_around(bv))
            bt = jnp.arange(n).reshape(w, WINDOW)
            btp = jnp.pad(bt, ((1, 0), (0, 0)), constant_values=-1)
            btk = jnp.concatenate([btp[:w], btp[1:]], axis=1)
            sim = jnp.einsum('bhwid,bhwjd->bhwij', bq, bk)
            i = bt[:, :, None]
            j = btk[:, None, :]
            mask = (i < j) | (i > j + WINDOW) | (j == -1)
            sim = jnp.where(mask, -jnp.finfo(sim.dtype).max, sim)
            attn = jax.nn.softmax(sim, axis=-1)
            out = jnp.einsum('bhwij,bhwjd->bhwid', attn, bv)
            return out.reshape(b, h, n, d)

        def _layer(x, wqkv, qs, ksc, wo, lg, lb, w1, b1, w2, b2):
            b, n, _ = x.shape
            h = shift_token(x)
            qkv = h @ wqkv
            q, k, v = jnp.split(qkv, 3, axis=-1)
            to_heads = lambda t: t.reshape(b, n, HEADS, DIM_HEAD).transpose(0, 2, 1, 3)
            q, k, v = (to_heads(q), to_heads(k), to_heads(v))
            q = l2norm(q) * qs
            k = l2norm(k) * ksc
            q, k = rotary_xpos(q, k)
            o = local_attention(q, k, v)
            o = o.transpose(0, 2, 1, 3).reshape(b, n, INNER)
            x = x + o @ wo
            h = shift_token(x)
            mu = h.mean(-1, keepdims=True)
            var = h.var(-1, keepdims=True)
            h = (h - mu) / jnp.sqrt(var + 1e-05) * lg + lb
            h = h @ w1 + b1
            a, g = jnp.split(h, 2, axis=-1)
            h = a * jax.nn.gelu(g, approximate=False)
            x = x + h @ w2 + b2
            return x
        for l in range(DEPTH):
            x = _layer(x, wqkv[l], q_scale[l], k_scale[l], wo[l], ln_g[l], ln_b[l], w1[l], b1[l], w2[l], b2[l])
        return x
    x = L0_attn_x
    xn = _layernorm(x, axis=-1)
    s = _L0_attn_ref(xn, L0_attn_norm_g, L0_attn_Wq, L0_attn_Wkv, L0_attn_Wout, L0_attn_out_norm_g)
    g = _silu(_L0_ffn_ref(xn, L0_ffn_wqkv, L0_ffn_q_scale, L0_ffn_k_scale, L0_ffn_wo, L0_ffn_ln_g, L0_ffn_ln_b, L0_ffn_w1, L0_ffn_b1, L0_ffn_w2, L0_ffn_b2))
    x = x + s * g
    return x

_drawn_inputs = setup_inputs


def setup_inputs(seed=0):
    import zlib

    import numpy as np

    out = dict(_drawn_inputs(seed))
    spreads = {'L0_attn_norm_g': (1.0, 0.2),
     'L0_attn_out_norm_g': (1.0, 0.2),
     'L0_ffn_q_scale': (1.0, 0.6),
     'L0_ffn_k_scale': (1.0, 0.6),
     'L0_ffn_ln_g': (1.0, 0.6),
     'L0_ffn_ln_b': (0.0, 0.8),
     'L0_ffn_b1': (0.0, 0.8),
     'L0_ffn_b2': (0.0, 0.322)}
    factors = {'L0_ffn_wqkv': 3.616, 'L0_ffn_wo': 3.615, 'L0_ffn_w1': 5.562, 'L0_ffn_w2': 5.485}
    for name, (base, spread) in spreads.items():
        noise = np.random.default_rng([zlib.crc32(name.encode()), seed]).standard_normal(out[name].shape)
        drawn = base * np.exp(spread * noise) if base else spread * noise
        out[name] = jnp.asarray(drawn.astype(out[name].dtype))
    for name, factor in factors.items():
        out[name] = (out[name] * factor).astype(out[name].dtype)
    return out
```

```python
import concourse.bass as bass
from concourse import mybir
from contextlib import ExitStack

import numpy as np


def gated_mqa_local_block(nc, x, norm_g, wq, wkv, wout, out_norm_g, wqkv, q_scale, k_scale, wo, ln_g, ln_b,
                          w1, b1, w2, b2, rope, ident_in, identh_in, shift_in, mask_in, keep_in, out):
    f32, f32r, f16, bf16 = mybir.dt.float32, mybir.dt.float32r, mybir.dt.float16, mybir.dt.bfloat16
    ALU, ACT, AX = mybir.AluOpType, mybir.ActivationFunctionType, mybir.AxisListType

    P = 128
    B, N, DIM = x.shape
    TILES = B * N // P
    TB = N // P
    DEPTH, _, QKV = wqkv.shape
    INNER = QKV // 3
    DH = q_scale.shape[1]
    HEADS = INNER // DH
    PAIRS = HEADS // 2
    HID = w2.shape[1]
    CH = -(-HID // P)
    TAIL = HID - (CH - 1) * P
    GROUP = 4
    HALF = P // 2
    HV = DH + 1
    VW = 2 * DH + 2
    EPS = 1e-5
    TINY = 1e-24
    QS = 64.0
    HG = 4
    UNITS = HEADS // HG
    ATT_SCALE = 16.0 / (QS * QS)

    with ExitStack() as ctx:
        def sb(name, shape, dt=f32):
            return ctx.enter_context(nc.sbuf_tensor(name, shape, dt))

        def sem(name):
            return ctx.enter_context(nc.semaphore(name))

        wq_sb = sb("wq_sb", [P, INNER])
        wkv_sb = sb("wkv_sb", [P, 2 * DH])
        wout_sb = sb("wout_sb", [P, PAIRS, DIM])
        wqkv_sb = sb("wqkv_sb", [P, DEPTH, QKV])
        wo_sb = sb("wo_sb", [P, DEPTH, PAIRS, DIM])
        w1_sb = sb("w1_sb", [P, 2 * HID])
        w2_sb = sb("w2_sb", [P, DEPTH, CH, DIM])
        b1_sb = sb("b1_sb", [P, DEPTH, 2, CH])
        lng_sb = sb("lng_sb", [P, DEPTH])
        lnb_sb = sb("lnb_sb", [P, DEPTH])
        ng_sb = sb("ng_sb", [P, 1])
        og_sb = sb("og_sb", [P, DIM])
        qk_scale = sb("qk_scale", [P, DEPTH, 4, DH])
        rope_sb = sb("rope_sb", [P, 4, TB, DH])
        table = sb("table", [P, DEPTH, TB, 4, DH])
        ident = sb("ident", [P, P])
        shift = sb("shift", [P, 2, P])
        identb = sb("identb", [P, P], bf16)
        identh = sb("identh", [P, P], f16)
        mask = sb("mask", [P, TB, P], bf16)
        keep = sb("keep", [P, 2])
        neg_half = sb("neg_half", [P, 2 * HEADS])
        x_in = sb("x_in", [P, TILES, DIM])
        xs = sb("xs", [P, TILES, DIM])
        x1 = sb("x1", [P, B * (TB + 1), DIM])
        xnn = sb("xnn", [P, TILES, DIM])
        bn = sb("bn", [P, TILES, 6])
        mean = sb("mean", [P, TILES])
        scr = sb("scr", [P, 3, TILES])
        var = sb("var", [P, TILES])
        rstd = sb("rstd", [P, TILES])
        qT16 = sb("qT16", [P, TILES, HEADS, P], f16)
        kT16 = sb("kT16", [P, TILES, 2, P], f16)
        v_r = sb("v_r", [P, TILES, VW], f32r)
        aT = sb("aT", [P, 2, P])
        xst = sb("xst", [P, 2, P])
        sq = sb("sq", [P, 2 * INNER])
        ss = sb("ss", [P, 2 * HEADS])
        rn = sb("rn", [P, 2 * HEADS])
        qn = sb("qn", [P, 2 * INNER])
        q16 = sb("q16", [P, 2, HEADS, 2, DH], f16)
        k16 = sb("k16", [P, 2, 2, 2, DH], f16)
        p32 = sb("p32", [P, 2, 1024])
        p_hi = sb("p_hi", [P, 2, 1024], f32r)
        p_lo = sb("p_lo", [P, 2, 1024], f32r)
        oa = sb("oa", [P, HEADS, DH])
        oaT = sb("oaT", [P, PAIRS, P])
        rden = sb("rden", [P, HEADS])
        hT = sb("hT", [P, 2, P + 1])
        rot = sb("rot", [P, 2 * INNER])
        rqk = sb("rqk", [P, 2, 2 * INNER])
        t1 = sb("t1", [P, 2 * INNER])
        qT = sb("qT", [P, PAIRS, P])
        kT = sb("kT", [P, 2, PAIRS, P])
        mx = sb("mx", [P, HEADS])
        o_dummy = sb("o_dummy", [P, 1])
        frd = sb("frd", [P, HEADS])
        fbn = sb("fbn", [P, GROUP, 6])
        fmean = sb("fmean", [P, GROUP])
        fscr = sb("fscr", [P, 3, GROUP])
        fvar = sb("fvar", [P, GROUP])
        frs = sb("frs", [P, GROUP])
        h2T = sb("h2T", [P, GROUP * P])

        free = qT16[:, :, :, :].rearrange("p t h n -> p (t h n)").bitcast(f32)
        at = [0]

        def reused(*shape):
            n = int(np.prod(shape))
            view = free[:, at[0]:at[0] + n]
            at[0] += n
            names = "abc"[:len(shape)]
            return view.rearrange(f"p ({' '.join(names)}) -> p {' '.join(names)}", **dict(zip(names, shape)))

        v_own = reused(GROUP, HEADS, HV)
        v_mix = reused(GROUP, HEADS, HV)
        gT = reused(CH, GROUP * P)
        o, oT = reused(1, INNER)[:, 0, :], reused(PAIRS, P)
        h2, h2n = reused(GROUP, DIM), reused(GROUP, DIM)
        pr = p32
        flat = kT16[:, :, :, :].rearrange("p t k n -> p (t k n)").bitcast(f32)
        sc = flat[:, 0:HEADS * P]
        prT = flat[:, HEADS * P:2 * HEADS * P].rearrange("p (h n) -> p h n", n=P)
        gl = rope_sb[:, :, :, :].rearrange("p f t d -> p (f t d)")[:, 0:CH * GROUP * P]\
            .rearrange("p (c n) -> p c n", c=CH)

        ps = [ctx.enter_context(nc.psum_tensor(f"ps{i}", [P, 1024], f32)) for i in range(4)]

        s_w = sem("s_w")
        s_x = sem("s_x")
        s_w1 = sem("s_w1")
        s_out = sem("s_out")
        dch = sem("dch")
        s_init = sem("s_init")
        s_pow = sem("s_pow")
        s_pq = sem("s_pq")
        s_tab = sem("s_tab")
        a_st = sem("a_st")
        a_T = sem("a_T")
        a_Ts = sem("a_Ts")
        n_done = sem("n_done")
        a_proj = sem("a_proj")
        a_sq = sem("a_sq")
        a_split = sem("a_split")
        a_tr = sem("a_tr")
        a_trs = sem("a_trs")
        a_qk = sem("a_qk")
        a_exp = sem("a_exp")
        a_hl = sem("a_hl")
        a_pv = sem("a_pv")
        a_hi = sem("a_hi")
        a_or = sem("a_or")
        a_o = sem("a_o")
        a_oT = sem("a_oT")
        a_oTs = sem("a_oTs")
        a_wo = sem("a_wo")
        a_lin = sem("a_lin")
        f_st = sem("f_st")
        f_xT = sem("f_xT")
        f_hT = sem("f_hT")
        f_proj = sem("f_proj")
        f_sq = sem("f_sq")
        f_v = sem("f_v")
        f_n = sem("f_n")
        f_c = sem("f_c")
        f_rope = sem("f_rope")
        f_tr = sem("f_tr")
        f_trs = sem("f_trs")
        f_s = sem("f_s")
        f_sub = sem("f_sub")
        f_exp = sem("f_exp")
        f_pT = sem("f_pT")
        f_pTs = sem("f_pTs")
        f_pv = sem("f_pv")
        f_o = sem("f_o")
        f_oT = sem("f_oT")
        f_oTs = sem("f_oTs")
        f_wo = sem("f_wo")
        f_x1 = sem("f_x1")
        m_sh = sem("m_sh")
        m_n = sem("m_n")
        m_T = sem("m_T")
        m_Ts = sem("m_Ts")
        m_u = sem("m_u")
        m_g = sem("m_g")
        m_h = sem("m_h")
        m_d = sem("m_d")
        m_x = sem("m_x")
        e_e = sem("e_e")

        START = 1
        counters = [a_T, a_Ts, a_exp, a_hi, a_hl, a_lin, a_o, a_oT, a_oTs, a_or,
                    a_proj, a_pv, a_qk, a_split, a_sq, a_st, a_tr, a_trs, a_wo, f_c, f_exp, f_hT,
                    f_n, f_o, f_oT, f_oTs, f_pT, f_pTs, f_proj, f_pv, f_rope, f_s, f_sq, f_st, f_sub, f_tr, f_trs, f_v, f_wo, f_x1, f_xT, m_T, m_Ts,
                    m_d, m_g, m_h, m_n, m_sh, m_u, m_x]

        block = ctx.enter_context(nc.Block())

        N_W = 16 * (17 + DEPTH * (9 + 2 * CH))
        CPU = TB // 2
        CPT = UNITS * CPU
        AHEAD = 2

        def tiles_of_a(eng, pair, kbase=None):
            def body(tile, first, last):
                for j in range(CPT):
                    if j + AHEAD < CPT:
                        pair("scores", tile, j + AHEAD)
                    elif not last:
                        pair("scores", tile + 1, j + AHEAD - CPT)
                    pair("values", tile, j)
                    if j == 2 and not first:
                        pair("finish", tile - 1, 0)
                if last:
                    pair("finish", tile, 0)

            with eng.Fori(0, B) as b:
                t0 = b * TB
                if kbase is not None:
                    kbase[0] = t0
                for j in range(AHEAD):
                    pair("scores", t0, j)
                body(t0, True, False)
                with eng.Fori(1, TB - 1) as i:
                    body(t0 + i, False, False)
                body(t0 + TB - 1, False, True)

        def schedule():
            for s in range(-2, GROUP):
                if 0 <= s + 1 < GROUP:
                    yield "scores", s + 1
                if 0 <= s + 2 < GROUP:
                    yield "project", s + 2
                if 0 <= s:
                    yield "values", s
                if 0 <= s + 2 < GROUP:
                    yield "rope", s + 2
                if 0 <= s:
                    yield "output", s

        def reuse(n0, u, depth):
            return n0 + max(0, u - depth + 1)

        @block.sync
        def _(sp):
            for counter in counters:
                sp.sem_inc(counter, 1)
            for c in range(4):
                t = TILES // 4
                b, o0 = divmod(c * t, TB)
                sp.dma_start(x_in[:, c * t:(c + 1) * t, :],
                             x[b, o0 * P:(o0 + t) * P, :].rearrange("(t p) d -> p t d", p=P)).then_inc(s_x, 16)
            loads = [
                (ident[:, :], ident_in), (ng_sb[:, :], norm_g.rearrange("(p o) -> p o", o=1)),
                (wq_sb[:, :], wq), (wkv_sb[:, :], wkv),
                (identb[:, :], mask_in[0]), (identh[:, :], identh_in),
                (wout_sb[:, :, :], wout.rearrange("(c p) n -> p c n", p=P)),
                (og_sb[:, :], out_norm_g.rearrange("(o d) -> o d", o=1).to_broadcast([P, DIM])),
                (wqkv_sb[:, :, :], wqkv.rearrange("l p n -> p l n")),
                (wo_sb[:, :, :, :], wo.rearrange("l (c p) n -> p l c n", p=P)),
                (rope_sb[:, :, :, :], rope.rearrange("f (t p) d -> p f t d", p=P)),
                (mask[:, 0:1, :], mask_in[1:2].rearrange("t p n -> p t n")),
                (mask[:, 1:TB, :], mask_in[2:3].rearrange("t p n -> p t n").to_broadcast([P, TB - 1, P])),
                (shift[:, :, :], shift_in.rearrange("t p n -> p t n")),
                (keep[:, :], keep_in),
                (lng_sb[:, :], ln_g), (lnb_sb[:, :], ln_b),
            ]
            for l in range(DEPTH):
                loads += [
                    (w2_sb[:, l, 0:CH - 1, :], w2[l, 0:(CH - 1) * P, :].rearrange("(c p) n -> p c n", p=P)),
                    (w2_sb[0:TAIL, l, CH - 1, :], w2[l, (CH - 1) * P:HID, :]),
                    (w2_sb[TAIL:TAIL + 1, l, CH - 1, :], b2[l:l + 1, :]),
                ]
                for k, v in ((0, q_scale), (1, k_scale)):
                    row = v[l:l + 1, :]
                    loads += [(qk_scale[:, l, k, :], row.to_broadcast([P, DH])),
                              (qk_scale[:, l, 2 + k, 0:DH // 2], row[:, DH // 2:DH].to_broadcast([P, DH // 2])),
                              (qk_scale[:, l, 2 + k, DH // 2:DH], row[:, 0:DH // 2].to_broadcast([P, DH // 2]))]
                for k in range(2):
                    for c in range(CH):
                        rows = P if c < CH - 1 else TAIL
                        at0 = k * HID + c * P
                        loads += [(b1_sb[0:rows, l, k, c:c + 1],
                                   b1[l, at0:at0 + rows].rearrange("(p o) -> p o", o=1))]
            assert 16 * len(loads) == N_W
            for dst, src in loads:
                sp.dma_start(dst, src).then_inc(s_w, 16)
            with sp.Fori(0, DEPTH) as l:
                sp.wait_ge(m_u, START + l * (TILES // GROUP) * 2 * CH)
                sp.dma_start(w1_sb[:, :], w1[l]).then_inc(s_w1, 16)
            sp.wait_ge(e_e, 2)
            for c in range(4):
                t = TILES // 4
                b, o0 = divmod(c * t, TB)
                sp.dma_start(out[b, o0 * P:(o0 + t) * P, :].rearrange("(t p) d -> p t d", p=P),
                             xs[:, c * t:(c + 1) * t, :]).then_inc(s_out, 16)
            sp.wait_ge(s_out, 64)

        @block.gpsimd
        def _(pool):
            pool.memset(neg_half[:, :], -0.5)
            pool.memset(x1[:, 0, :], 0.0)
            pool.memset(x1[:, TB + 1, :], 0.0)
            pool.memset(hT[:, :, :], 0.0)
            pool.memset(kT[:, :, :, :], 0.0)
            pool.memset(qn[:, 0:16 * 2], 0.0)
            pool.memset(p32[:, 0, 0:TILES], 1.0)
            pool.memset(p32[:, 0, TILES:2 * TILES], 0.0).then_inc(s_init, 1)
            for k in range(2):
                pool.wait_ge(s_pq, k + 1)
                pool.tensor_tensor(rstd[:, :], var[:, :], neg_half[:, 0:TILES], ALU.pow).then_inc(s_pow, 1)
            pool.wait_ge(s_w, N_W)
            for l in range(DEPTH):
                for f in range(4):
                    last = pool.tensor_tensor(table[:, l, :, f, :], rope_sb[:, f, :, :],
                                              qk_scale[:, l, f:f + 1, :].to_broadcast([P, TB, DH]), ALU.mult)
            last.then_inc(s_tab, 1)
            with pool.Fori(0, TILES) as t:
                pool.wait_ge(s_pq, t + 3)
                pool.tensor_tensor(rn[:, 0:HEADS + 1], ss[:, 0:HEADS + 1], neg_half[:, 0:HEADS + 1],
                                   ALU.pow).then_inc(s_pow, 1)
            pool.wait_ge(s_pq, TILES + 3)
            pool.tensor_tensor(rstd[:, :], var[:, :], neg_half[:, 0:TILES], ALU.pow).then_inc(s_pow, 1)
            pool.memset(v_mix[:, :, :, :], 0.0).then_inc(s_init, 1)
            pool.memset(gT[:, :, :], 1.0)
            pool.memset(v_own[:, :, :, DH:HV], 1.0)
            pool.wait_ge(s_init, 2)
            pool.memset(v_mix[:, :, :, DH:HV], 1.0).then_inc(s_init, 1)
            R0 = TILES + 3
            RG = GROUP + 1

            def project(u, n0, g, ask):
                pool.wait_ge(s_pq, R0 + g * RG + u + 1)
                pool.tensor_tensor(rn[:, :], ss[:, :], neg_half[:, :], ALU.pow).then_inc(s_pow, 1)

            def rope_(u, n0, l, half):
                pool.wait_ge(f_n, START + n0 + u + 1)
                src = qn[:, :].rearrange("p (k h d) -> p k h d", k=2, d=DH)
                dst = rot[:, :].rearrange("p (k h d) -> p k h d", k=2, d=DH)
                hd = DH // 2
                for k in range(2):
                    for a, c in ((0, hd), (hd, 0)):
                        last = pool.tensor_tensor(
                            dst[:, k, :, a:a + hd], src[:, k, :, c:c + hd],
                            table[:, l, half * GROUP + u, 2 + k:3 + k, a:a + hd].to_broadcast([P, HEADS, hd]), ALU.mult)
                last.then_inc(f_c, 1)

            with pool.Fori(0, DEPTH) as l, pool.Fori(0, B) as b, pool.Fori(0, TB // GROUP) as half:
                g = l * (TILES // GROUP) + b * (TB // GROUP) + half
                n0 = g * GROUP
                for stage, u in schedule():
                    if stage == "project":
                        project(u, n0, g, None)
                    elif stage == "rope":
                        rope_(u, n0, l, half)
                pool.wait_ge(s_pq, R0 + g * RG + RG)
                pool.tensor_tensor(frs[:, :], fvar[:, :], neg_half[:, 0:GROUP], ALU.pow).then_inc(s_pow, 1)

        @block.scalar
        def _(act):
            act.wait_ge(s_w, N_W)
            g_of = [0]
            act.activation(o_dummy[:, 0:1], keep[:, 0:1], ACT.Exp).then_inc(a_exp, 1)

            def front(t, u):
                act.wait_ge(a_T, START + t)
                act.wait_ge(n_done, 1)
                act.activation(xst[:, u, :], xnn[:, t, :], ACT.Copy).then_inc(a_st, 1)
                act.wait_ge(a_T, START + t + 1)
                act.activation(aT[:, u, :], ps[3][:, 0:P], ACT.Copy, scale=ng_sb[:, 0:1]).then_inc(a_Ts, 1)
                act.wait_ge(a_proj, START + t + 1)
                act.wait_ge(s_pq, t + 2)
                act.activation(sq[:, 0:INNER + DH], ps[u][:, 0:INNER + DH], ACT.Square).then_inc(a_sq, 1)

            def back(t, u):
                act.wait_ge(a_tr, START + t + 1)
                act.activation(qT16[:, t, :, :], ps[2][:, 0:512].bitcast(f16), ACT.Copy)
                act.activation(kT16[:, t, :, :], ps[2][:, 512:640].bitcast(f16), ACT.Copy).then_inc(a_trs, 1)

            front(0, 0)
            with act.Fori(0, TILES // 2 - 1) as i:
                front(i * 2 + 1, 1)
                back(i * 2, 0)
                front(i * 2 + 2, 0)
                back(i * 2 + 1, 1)
            front(TILES - 1, 1)
            back(TILES - 2, 0)
            back(TILES - 1, 1)

            def attend(event, tile, j):
                if event == "scores":
                    chunk = tile * CPT + j
                    act.wait_ge(a_qk, START + chunk + 1)
                    act.wait_ge(a_hl, START + chunk)
                    act.activation(p32[:, j % 2, :], ps[j % 2][:, :], ACT.Exp, scale=ATT_SCALE).then_inc(a_exp, 1)
                elif event == "finish":
                    act.wait_ge(a_oT, START + tile + 1)
                    act.activation(oaT[:, :, :], ps[3][:, 0:512], ACT.Copy).then_inc(a_oTs, 1)

            tiles_of_a(act, attend)

            def project(u, n0, tile):
                n = n0 + u
                act.wait_ge(m_x, START + g_of[0])
                act.wait_ge(f_xT, START + reuse(n0, u, 2))
                act.activation(xst[:, u % 2, :], xs[:, tile, :], ACT.Copy).then_inc(f_st, 1)
                act.wait_ge(f_proj, START + n + 1)
                act.wait_ge(s_pq, TILES + 3 + g_of[0] * (GROUP + 1) + u)
                act.activation(sq[:, :], ps[0][:, :], ACT.Square).then_inc(f_sq, 1)
                src = ps[3][:, 0:INNER].rearrange("p (h d) -> p h d", d=DH)
                act.wait_ge(s_init, 3)
                act.wait_ge(f_pv, START + reuse(n0, u, 3))
                act.activation(v_own[:, u, :, 0:DH], src, ACT.Copy)
                act.activation(v_mix[0:HALF, u, :, 0:DH], src[0:HALF], ACT.Copy)
                act.activation(v_mix[HALF:P, (u + 1) % GROUP, :, 0:DH], src[HALF:P], ACT.Copy).then_inc(f_v, 1)

            def scores(u, n0):
                n = n0 + u
                act.wait_ge(f_tr, START + n + 1)
                act.wait_ge(f_s, START + n)
                act.activation(qT[:, :, :], ps[1][:, 0:512], ACT.Copy)
                act.activation(kT[:, u % 2, :, :], ps[1][:, 512:1024], ACT.Copy).then_inc(f_trs, 1)
                act.wait_ge(f_sub, START + n + 1)
                act.wait_ge(f_pT, START + reuse(n0, u, 2))
                act.activation(pr[:, u % 2, :], sc[:, :], ACT.Exp).then_inc(f_exp, 1)

            def values(u, n0):
                act.wait_ge(f_pT, START + n0 + u + 1)
                act.activation(prT[:, :, :], ps[1][:, :], ACT.Copy).then_inc(f_pTs, 1)

            def output(u, n0):
                act.wait_ge(f_oT, START + n0 + u + 1)
                act.activation(oT[:, :, :], ps[3][:, 512:1024], ACT.Copy).then_inc(f_oTs, 1)

            with act.Fori(0, DEPTH) as l, act.Fori(0, B) as b, act.Fori(0, TB // GROUP) as half:
                g = l * (TILES // GROUP) + b * (TB // GROUP) + half
                n0 = g * GROUP
                g_of[0] = g
                for stage, u in schedule():
                    if stage == "project":
                        project(u, n0, b * TB + half * GROUP + u)
                    elif stage == "scores":
                        scores(u, n0)
                    elif stage == "values":
                        values(u, n0)
                    elif stage == "output":
                        output(u, n0)
                act.wait_ge(m_T, START + g + 1)
                act.activation(h2T[:, :], ps[3][:, 0:512], ACT.Identity, scale=lng_sb[:, bass.ds(l, 1)],
                               bias=lnb_sb[:, bass.ds(l, 1)]).then_inc(m_Ts, 1)
                for c in range(CH):
                    rows = P if c < CH - 1 else TAIL
                    act.wait_ge(m_u, START + g * 2 * CH + 2 * c + 2)
                    act.activation(gl[0:rows, c, :], ps[c][0:rows, 512:1024], ACT.Gelu,
                                   bias=b1_sb[0:rows, l, 1, c:c + 1]).then_inc(m_g, 1)
            act.wait_ge(m_x, START + DEPTH * TILES // GROUP)
            act.activation(p32[:, :, :], xs[:, :, :].rearrange("p t d -> p (t d)").rearrange("p (a b) -> p a b", a=2),
                           ACT.Exp, scale=-1.0).then_inc(e_e, 1)

        @block.vector
        def _(dve):
            DVE = nc.vector

            class Chain:
                base = 0
                n = 0

            ch = Chain()

            def link(ins):
                ch.n += 1
                ins.then_inc(dch, 1)
                dve.wait_ge(dch, ch.base + ch.n)

            def statistics(stats, mean, variance, scratch):
                m0, m1, q0, q1 = (stats[:, :, c] for c in (1, 4, 2, 5))
                d, d2, m2 = (scratch[:, c, :] for c in range(3))
                DVE.tensor_tensor(mean, m0, m1, ALU.add)
                DVE.tensor_tensor(d, m0, m1, ALU.subtract)
                link(DVE.tensor_tensor(m2, q0, q1, ALU.add))
                DVE.tensor_scalar(mean, mean, 0.5, None, ALU.mult)
                DVE.tensor_scalar(m2, m2, 1.0 / DIM, EPS, ALU.mult, ALU.add)
                link(DVE.scalar_tensor_tensor(d2, d, 0.25, d, ALU.mult, ALU.mult))
                return DVE.tensor_tensor(variance, m2, d2, ALU.add)

            def norm(dst, src, k):
                if k == 0:
                    dve.wait_ge(s_x, 64)
                with dve.Fori(0, TILES) as t:
                    DVE.bn_stats(bn[:, t, :], src[:, t, :]).then_inc(dch, 1)
                ch.base = ch.base + TILES
                dve.wait_ge(dch, ch.base + ch.n)
                statistics(bn, mean[:, :], var[:, :], scr).then_inc(s_pq, 1)
                dve.wait_ge(s_pow, k + 1)
                with dve.Fori(0, TILES) as t:
                    DVE.tensor_scalar(dst[:, t, :], src[:, t, :], mean[:, bass.ds(t, 1)], rstd[:, bass.ds(t, 1)],
                                      ALU.subtract, ALU.mult).then_inc(dch, 1)
                ch.base = ch.base + TILES
                dve.wait_ge(dch, ch.base + ch.n)

            dve.wait_ge(s_init, 1)
            DVE.tensor_copy(v_r[:, :, 2 * DH:VW - 1], p32[:, 0, 0:TILES].unsqueeze(2))
            DVE.tensor_copy(v_r[:, :, VW - 1:VW], p32[:, 0, TILES:2 * TILES].unsqueeze(2)).then_inc(a_split, 1)
            norm(xs, x_in, 0)
            norm(xnn, xs, 1)
            DVE.memset(mx[:, 0:1], 0.0).then_inc(n_done, 1)
            ch.base, ch.n = ch.base + ch.n, 0
            A_STEPS = 6
            with dve.Fori(0, TILES // 2) as i:
                base0 = ch.base
                for u in range(2):
                    t = i * 2 + u
                    base = base0 + i * 2 * A_STEPS + u * A_STEPS
                    dve.wait_ge(a_sq, START + t + 1)
                    DVE.tensor_reduce(ss[:, 0:HEADS + 1], sq[:, 0:INNER + DH].rearrange("p (h d) -> p h d", d=DH),
                                      AX.X, ALU.add).then_inc(dch, 1)
                    dve.wait_ge(dch, base + 1)
                    DVE.tensor_scalar(ss[:, 0:HEADS + 1], ss[:, 0:HEADS + 1], TINY, None, ALU.max).then_inc(s_pq, 1)
                    dve.wait_ge(s_pow, t + 3)
                    DVE.tensor_scalar(rn[:, 0:HEADS + 1], rn[:, 0:HEADS + 1], QS, None, ALU.mult).then_inc(dch, 1)
                    dve.wait_ge(dch, base + 2)
                    q_ps = ps[u][:, 0:INNER + DH].rearrange("p (h d) -> p h d", d=DH)
                    DVE.tensor_tensor(qn[:, 0:INNER + DH].rearrange("p (h d) -> p h d", d=DH), q_ps,
                                      rn[:, 0:HEADS + 1].unsqueeze(2).to_broadcast([P, HEADS + 1, DH]),
                                      ALU.mult).then_inc(dch, 1)
                    DVE.tensor_copy(v_r[:, t, 0:DH], ps[u][:, INNER + DH:INNER + 2 * DH]).then_inc(dch, 1)
                    dve.wait_ge(dch, base + 4)
                    DVE.tensor_tensor(v_r[:, t, DH:2 * DH], ps[u][:, INNER + DH:INNER + 2 * DH],
                                      v_r[:, t, 0:DH].bitcast(f32), ALU.subtract).then_inc(dch, 1)
                    dve.wait_ge(a_tr, START + i * 2)
                    qf = qn[:, 0:INNER].rearrange("p (h d) -> p h d", d=DH)
                    kf = qn[:, INNER:INNER + DH]
                    DVE.tensor_copy(q16[:, u, :, 0, :], qf)
                    DVE.tensor_copy(k16[:, u, 0, 0, :], kf)
                    DVE.tensor_copy(k16[:, u, 1, 1, :], kf).then_inc(dch, 1)
                    dve.wait_ge(dch, base + 6)
                    DVE.tensor_tensor(q16[:, u, :, 1, :], qf, q16[:, u, :, 0, :], ALU.subtract)
                    DVE.tensor_tensor(k16[:, u, 0, 1, :], kf, k16[:, u, 0, 0, :], ALU.subtract)
                    DVE.tensor_tensor(k16[:, u, 1, 0, :], kf, k16[:, u, 0, 0, :], ALU.subtract).then_inc(a_split, 1)
            ch.base = ch.base + TILES * A_STEPS

            def attend(event, tile, j):
                if event == "scores":
                    chunk = tile * CPT + j
                    dve.wait_ge(a_exp, START + chunk + 2)
                    dve.wait_ge(a_pv, START + chunk)
                    DVE.tensor_copy(p_hi[:, j % 2, :], p32[:, j % 2, :]).then_inc(a_hi, 1)
                    dve.wait_ge(a_hi, START + chunk + 1)
                    DVE.tensor_tensor(p_lo[:, j % 2, :], p32[:, j % 2, :], p_hi[:, j % 2, :].bitcast(f32),
                                      ALU.subtract).then_inc(a_hl, 1)
                elif event == "values" and j % CPU == CPU - 1:
                    hg = j // CPU
                    unit = tile * UNITS + hg
                    dve.wait_ge(a_pv, START + (unit + 1) * CPU + 1)
                    if hg == 0:
                        dve.wait_ge(a_oT, START + tile)
                    pv = ps[2][:, :].rearrange("p (k n) -> p k n", k=2)[:, :, 0:2 * VW]\
                        .rearrange("p k (h v) -> p k h v", v=VW)
                    DVE.reciprocal(rden[:, 0:HG].rearrange("p (k h) -> p k h", k=2), pv[:, :, :, 2 * DH])
                    for k in range(2):
                        h0 = hg * HG + 2 * k
                        last = DVE.tensor_reduce(oa[:, h0:h0 + 2, :],
                                                 pv[:, k, :, 0:2 * DH].rearrange("p h (a d) -> p h d a", a=2),
                                                 AX.X, ALU.add)
                    last.then_inc(a_or, 1)
                    dve.wait_ge(a_or, START + unit + 1)
                    hs = slice(hg * HG, (hg + 1) * HG)
                    DVE.tensor_tensor(oa[:, hs, :], oa[:, hs, :],
                                      rden[:, 0:HG].unsqueeze(2).to_broadcast([P, HG, DH]),
                                      ALU.mult).then_inc(a_o, 1)
                elif event == "finish":
                    dve.wait_ge(a_wo, START + tile + 1)
                    DVE.tensor_scalar(xnn[:, tile, :], ps[3][:, 512:512 + DIM], 1.0, None, ALU.mult)
                    DVE.bn_stats(bn[:, tile, :], ps[3][:, 512:512 + DIM]).then_inc(a_lin, 1)

            DVE.memset(mx[:, 0:1], 0.0).then_inc(a_hl, 1)
            tiles_of_a(dve, attend)
            dve.wait_ge(a_lin, START + TILES)
            statistics(bn, mean[:, :], var[:, :], scr).then_inc(s_pq, 1)
            dve.wait_ge(s_pow, TILES + 3)
            with dve.Fori(0, TILES) as t:
                DVE.tensor_scalar(xnn[:, t, :], xnn[:, t, :], mean[:, bass.ds(t, 1)], rstd[:, bass.ds(t, 1)], ALU.subtract,
                                  ALU.mult).then_inc(dch, 1)
                dve.wait_ge(dch, ch.base + ch.n + t * 2 + 1)
                DVE.tensor_tensor(xnn[:, t, :], xnn[:, t, :], og_sb[:, :], ALU.mult).then_inc(dch, 1)
            ch.n += 2 * TILES
            dve.wait_ge(dch, ch.base + ch.n)
            ch.base, ch.n = ch.base + ch.n, 0

            R0 = TILES + 3
            RG = GROUP + 1
            F_STEPS = 4 * GROUP + 5
            dve.wait_ge(s_tab, 1)

            def project(u, n0, g, half):
                n = n0 + u
                dve.wait_ge(f_xT, START + n + 1)
                dve.wait_ge(f_proj, START + n)
                DVE.tensor_copy(hT[0:HALF, u % 2, 0:P], ps[3][0:HALF, 0:P])
                DVE.tensor_copy(hT[HALF:P, u % 2, 1:P + 1], ps[3][HALF:P, 0:P])
                nxt = hT[HALF:P, (u + 1) % 2, 0:1]
                if u < GROUP - 1:
                    DVE.tensor_copy(nxt, ps[3][HALF:P, P - 1:P]).then_inc(f_hT, 1)
                else:
                    DVE.tensor_scalar(nxt, ps[3][HALF:P, P - 1:P], keep[HALF:P, bass.ds(half, 1)], None,
                                      ALU.mult).then_inc(f_hT, 1)
                dve.wait_ge(f_sq, START + n + 1)
                link(DVE.tensor_reduce(ss[:, :], sq[:, :].rearrange("p (h d) -> p h d", d=DH), AX.X, ALU.add))
                DVE.tensor_scalar(ss[:, :], ss[:, :], TINY, None, ALU.max).then_inc(s_pq, 1)

            def rope_(u, n0, g, l, half):
                n = n0 + u
                dve.wait_ge(s_pow, R0 + g * RG + u + 1)
                dve.wait_ge(f_c, START + n)
                DVE.tensor_tensor(qn[:, :].rearrange("p (h d) -> p h d", d=DH),
                                  ps[0][:, :].rearrange("p (h d) -> p h d", d=DH),
                                  rn[:, :].unsqueeze(2).to_broadcast([P, 2 * HEADS, DH]), ALU.mult).then_inc(f_n, 1)
                dve.wait_ge(f_n, START + n + 1)
                for k in range(2):
                    last = DVE.tensor_tensor(
                        t1[:, :].rearrange("p (k h d) -> p k h d", k=2, d=DH)[:, k, :, :],
                        qn[:, :].rearrange("p (k h d) -> p k h d", k=2, d=DH)[:, k, :, :],
                        table[:, l, half * GROUP + u, k:k + 1, :].to_broadcast([P, HEADS, DH]), ALU.mult)
                link(last)
                dve.wait_ge(f_c, START + n + 1)
                dve.wait_ge(f_tr, START + reuse(n0, u, 2))
                DVE.tensor_tensor(rqk[:, u % 2, :], t1[:, :], rot[:, :], ALU.add).then_inc(f_rope, 1)

            def scores(u, n0):
                n = n0 + u
                dve.wait_ge(f_s, START + n + 1)
                s3 = ps[2][:, :].rearrange("p (h j) -> p h j", j=P)
                link(DVE.tensor_reduce(mx[:, :], s3, AX.X, ALU.max))
                dve.wait_ge(f_exp, START + n)
                DVE.tensor_tensor(sc[:, :].rearrange("p (h j) -> p h j", j=P), s3,
                                  mx[:, :].unsqueeze(2).to_broadcast([P, HEADS, P]), ALU.subtract).then_inc(f_sub, 1)

            def values(u, n0):
                n = n0 + u
                dve.wait_ge(f_pv, START + n + 1)
                pv = ps[1][:, :].rearrange("p (k n) -> p k n", k=2)[:, :, 0:PAIRS * HV]\
                    .rearrange("p k (h v) -> p k h v", v=HV)
                link(DVE.reciprocal(frd[:, :].rearrange("p (k h) -> p k h", k=2), pv[:, :, :, DH]))
                dve.wait_ge(f_oT, START + n)
                for k in range(2):
                    last = DVE.tensor_tensor(
                        o[:, k * INNER // 2:(k + 1) * INNER // 2].rearrange("p (h d) -> p h d", d=DH),
                        pv[:, k, :, 0:DH],
                        frd[:, k * PAIRS:(k + 1) * PAIRS].unsqueeze(2).to_broadcast([P, PAIRS, DH]), ALU.mult)
                last.then_inc(f_o, 1)

            def output(u, n0, b, half):
                n = n0 + u
                dve.wait_ge(f_wo, START + n + 1)
                tile = (b * (TB // GROUP) + half) * GROUP + u
                slot = b * (TB + 1) + half * GROUP + u + 1
                DVE.tensor_tensor(x1[:, slot, :], ps[3][:, 512:512 + DIM], xs[:, tile, :],
                                  ALU.add).then_inc(f_x1, 1)

            with dve.Fori(0, DEPTH) as l, dve.Fori(0, B) as b, dve.Fori(0, TB // GROUP) as half:
                g = l * (TILES // GROUP) + b * (TB // GROUP) + half
                n0 = g * GROUP
                base0, n_before = ch.base, ch.n
                ch.base, ch.n = base0 + g * F_STEPS, 0
                for stage, u in schedule():
                    if stage == "project":
                        project(u, n0, g, half)
                    elif stage == "rope":
                        rope_(u, n0, g, l, half)
                    elif stage == "scores":
                        scores(u, n0)
                    elif stage == "values":
                        values(u, n0)
                    elif stage == "output":
                        output(u, n0, b, half)
                slot = b * (TB + 1) + half * GROUP + 1
                dve.wait_ge(m_sh, START + g + 1)
                dve.wait_ge(f_x1, START + n0 + GROUP)
                DVE.tensor_scalar(h2[:, :, 0:HALF], x1[:, bass.ds(slot, GROUP), 0:HALF], 1.0, None, ALU.mult)
                link(DVE.tensor_copy(h2[:, :, HALF:P], ps[3][:, 0:GROUP * HALF]
                                     .rearrange("p (u d) -> p u d", d=HALF)))
                for u in range(GROUP):
                    last = DVE.bn_stats(fbn[:, u, :], h2[:, u, :])
                link(last)
                statistics(fbn, fmean[:, :], fvar[:, :], fscr).then_inc(s_pq, 1)
                dve.wait_ge(s_pow, R0 + g * RG + RG)
                for u in range(GROUP):
                    last = DVE.tensor_scalar(h2n[:, u, :], h2[:, u, :], fmean[:, u:u + 1], frs[:, u:u + 1],
                                             ALU.subtract, ALU.mult)
                last.then_inc(m_n, 1)
                for c in range(CH):
                    rows = P if c < CH - 1 else TAIL
                    dve.wait_ge(m_g, START + g * CH + c + 1)
                    DVE.scalar_tensor_tensor(gT[0:rows, c, :], ps[c][0:rows, 0:512], b1_sb[0:rows, l, 0, c:c + 1],
                                             gl[0:rows, c, :], ALU.add, ALU.mult).then_inc(m_h, 1)
                dve.wait_ge(m_d, START + g + 1)
                tile = (b * (TB // GROUP) + half) * GROUP
                DVE.tensor_tensor(xs[:, bass.ds(tile, GROUP), :], x1[:, bass.ds(slot, GROUP), :],
                                  ps[3][:, 0:GROUP * P].rearrange("p (u d) -> p u d", d=P),
                                  ALU.add).then_inc(m_x, 1)
                link(DVE.memset(mx[:, 0:1], 0.0))
                assert ch.n == F_STEPS, ch.n
                ch.base, ch.n = base0 + DEPTH * (TILES // GROUP) * F_STEPS, 0
            dve.wait_ge(e_e, 1)
            dve.wait_ge(m_x, START + DEPTH * TILES // GROUP)
            e = p32[:, :, :].rearrange("p a b -> p (a b)")
            xf, sf, xi = (t[:, :, :].rearrange("p t d -> p (t d)") for t in (xs, xnn, x_in))
            link(DVE.tensor_scalar(e, e, 1.0, None, ALU.add))
            link(DVE.reciprocal(e, e))
            link(DVE.tensor_tensor(xf, xf, e, ALU.mult))
            link(DVE.tensor_tensor(xf, xf, sf, ALU.mult))
            DVE.tensor_tensor(xf, xf, xi, ALU.add).then_inc(e_e, 1)

        @block.tensor
        def _(pe):
            PE = nc.tensor
            one = dict(start=True, stop=True)
            pe.wait_ge(s_w, N_W)
            pe.wait_ge(n_done, 1)


            def front(t, u):
                pe.wait_ge(a_st, START + t + 1)
                pe.wait_ge(a_Ts, START + t)
                PE.transpose(ps[3][:, 0:P], xst[:, u, :], ident[:, :]).then_inc(a_T, 1)
                pe.wait_ge(a_Ts, START + t + 1)
                pe.wait_ge(a_split, START + t)
                PE.matmul(ps[u][:, 0:INNER], aT[:, u, :], wq_sb[:, :], **one)
                PE.matmul(ps[u][:, INNER:INNER + 2 * DH], aT[:, u, :], wkv_sb[:, :], **one).then_inc(a_proj, 1)

            def back(t, u):
                pe.wait_ge(a_split, START + t + 2)
                pe.wait_ge(a_trs, START + t)
                for h in range(HEADS):
                    PE.transpose(ps[2][:, h * HALF:(h + 1) * HALF].bitcast(f16),
                                 q16[:, u, h, :, :].rearrange("p a d -> p (a d)"), identh[:, :])
                for k in range(2):
                    last = PE.transpose(ps[2][:, 512 + k * HALF:512 + (k + 1) * HALF].bitcast(f16),
                                        k16[:, u, k, :, :].rearrange("p a d -> p (a d)"), identh[:, :])
                last.then_inc(a_tr, 1)

            front(0, 0)
            with pe.Fori(0, TILES // 2 - 1) as i:
                front(i * 2 + 1, 1)
                back(i * 2, 0)
                front(i * 2 + 2, 0)
                back(i * 2 + 1, 1)
            front(TILES - 1, 1)
            back(TILES - 2, 0)
            back(TILES - 1, 1)
            pe.wait_ge(a_trs, START + TILES)
            PE.matmul(ps[3][:, 0:P], identh[:, :], identh[:, :], **one).then_inc(a_pv, 1)

            def attend(event, tile, j):
                chunk = tile * CPT + j
                hg, c = divmod(j, CPU)
                if event == "scores":
                    pe.wait_ge(a_exp, START + chunk)
                    for k in range(2):
                        for part in range(2):
                            last = PE.matmul(ps[j % 2][:, k * 512:(k + 1) * 512],
                                             kT16[:, kbase[0] + 2 * c + k, part, :],
                                             qT16[:, tile, hg * HG:(hg + 1) * HG, :],
                                             start=(part == 0), stop=(part == 1))
                    last.then_inc(a_qk, 1)
                elif event == "values":
                    if c == 0:
                        pe.wait_ge(a_o, START + tile * UNITS + hg)
                    pe.wait_ge(a_hl, START + chunk + 2)
                    for k in range(2):
                        for pi, part in enumerate((p_hi, p_lo)):
                            for h in range(HG):
                                col = (h // 2) * 512 + (h % 2) * VW
                                last = PE.matmul(
                                    ps[2][:, col:col + VW], part[:, j % 2, k * 512 + h * P:k * 512 + (h + 1) * P],
                                    v_r[:, kbase[0] + 2 * c + k, :],
                                    start=(c == 0 and k == 0 and pi == 0 and h % 2 == 0),
                                    stop=(c == CPU - 1 and k == 1 and pi == 1), skip_group_check=True)
                    last.then_inc(a_pv, 1)
                else:
                    pe.wait_ge(a_o, START + tile * UNITS + UNITS)
                    pe.wait_ge(a_lin, START + tile)
                    oflat = oa[:, :, :].rearrange("p h d -> p (h d)")
                    for k in range(PAIRS):
                        last = PE.transpose(ps[3][:, k * P:(k + 1) * P], oflat[:, k * P:(k + 1) * P], ident[:, :])
                    last.then_inc(a_oT, 1)
                    pe.wait_ge(a_oTs, START + tile + 1)
                    for k in range(PAIRS):
                        last = PE.matmul(ps[3][:, 512:512 + DIM], oaT[:, k, :], wout_sb[:, k, :],
                                         start=(k == 0), stop=(k == PAIRS - 1))
                    last.then_inc(a_wo, 1)

            kbase = [0]
            tiles_of_a(pe, attend, kbase)
            pe.wait_ge(a_lin, START + TILES)

            def project(u, n0, g):
                n = n0 + u
                pe.wait_ge(f_st, START + n + 1)
                pe.wait_ge(f_v, START + n)
                if u == 0:
                    pe.wait_ge(m_x, START + g)
                PE.transpose(ps[3][:, 0:P], xst[:, u % 2, :], ident[:, :]).then_inc(f_xT, 1)
                pe.wait_ge(f_hT, START + n + 1)
                pe.wait_ge(f_n, START + n)
                for k, dst in enumerate((ps[0][:, 0:512], ps[0][:, 512:1024], ps[3][:, 0:512])):
                    last = PE.matmul(dst, hT[:, u % 2, 0:P], wqkv_sb[:, lg[0], k * INNER:(k + 1) * INNER], **one)
                last.then_inc(f_proj, 1)

            def scores(u, n0):
                n = n0 + u
                pe.wait_ge(f_rope, START + n + 1)
                pe.wait_ge(f_o, START + n0 + max(0, u - 1))
                for k in range(2 * PAIRS):
                    last = PE.transpose(ps[1][:, k * P:(k + 1) * P], rqk[:, u % 2, k * P:(k + 1) * P], ident[:, :])
                last.then_inc(f_tr, 1)
                pe.wait_ge(f_trs, START + n + 1)
                pe.wait_ge(f_sub, START + n)
                for r in range(2):
                    PE.matmul(ps[2][:, r * 512:(r + 1) * 512].rearrange("p (h j) -> p h j", j=P), identb[:, :],
                              mask[:, bass.ds(tb[0] + u, 1), :].to_broadcast([P, PAIRS, P]),
                              start=True, stop=False, skip_group_check=True)
                rows = [slice(0, HALF), slice(HALF, P)]
                cur, prev = u % 2, (u + 1) % 2
                for k in range(PAIRS):
                    for r in range(2):
                        col = r * 512 + k * P
                        q, kc, kp = qT[rows[r], k, :], kT[rows[r], cur, k, :], kT[rows[r], prev, k, :]
                        acc = dict(start=False, stop=(k == PAIRS - 1), skip_group_check=True)
                        PE.matmul(ps[2][0:HALF, col:col + HALF], q[:, 0:HALF], kc[:, 0:HALF], **acc)
                        PE.matmul(ps[2][0:HALF, col + HALF:col + P], q[:, 0:HALF], kp[:, HALF:P], **acc)
                        last = PE.matmul(ps[2][HALF:P, col:col + P], q[:, HALF:P], kc, **acc)
                last.then_inc(f_s, 1)

            def values(u, n0):
                n = n0 + u
                pe.wait_ge(f_exp, START + n + 1)
                pe.wait_ge(f_trs, START + n + (2 if u < GROUP - 1 else 1))
                for k in range(HEADS):
                    last = PE.transpose(ps[1][:, k * P:(k + 1) * P], pr[:, u % 2, k * P:(k + 1) * P], ident[:, :])
                last.then_inc(f_pT, 1)
                pe.wait_ge(f_pTs, START + n + 1)
                for h in range(HEADS):
                    at = (h % 2) * PAIRS + h // 2
                    col = (h // PAIRS) * 512 + (h % PAIRS) * HV
                    PE.matmul(ps[1][0:HALF, col:col + HV], prT[:, at, 0:HALF], v_mix[:, u, h, :], **one)
                    last = PE.matmul(ps[1][HALF:P, col:col + HV], prT[:, at, HALF:P], v_own[:, u, h, :], **one)
                last.then_inc(f_pv, 1)

            def output(u, n0):
                n = n0 + u
                pe.wait_ge(f_o, START + n + 1)
                pe.wait_ge(f_x1, START + n)
                for k in range(PAIRS):
                    last = PE.transpose(ps[3][:, 512 + k * P:512 + (k + 1) * P], o[:, k * P:(k + 1) * P], ident[:, :])
                last.then_inc(f_oT, 1)
                pe.wait_ge(f_oTs, START + n + 1)
                for k in range(PAIRS):
                    last = PE.matmul(ps[3][:, 512:512 + DIM], oT[:, k, :], wo_sb[:, lg[0], k, :],
                                     start=(k == 0), stop=(k == PAIRS - 1))
                last.then_inc(f_wo, 1)

            lg, tb = [0], [0]
            with pe.Fori(0, DEPTH) as l, pe.Fori(0, B) as b, pe.Fori(0, TB // GROUP) as half:
                g = l * (TILES // GROUP) + b * (TB // GROUP) + half
                n0 = g * GROUP
                lg[0], tb[0] = l, half * GROUP
                for stage, u in schedule():
                    if stage == "project":
                        project(u, n0, g)
                    elif stage == "scores":
                        scores(u, n0)
                    elif stage == "values":
                        values(u, n0)
                    elif stage == "output":
                        output(u, n0)
                pe.wait_ge(f_x1, START + n0 + GROUP)
                pe.wait_ge(f_v, START + n0 + GROUP)
                slot = b * (TB + 1) + half * GROUP + 1
                for u in range(GROUP):
                    dst = ps[3][:, u * HALF:(u + 1) * HALF]
                    PE.matmul(dst, shift[:, 0, :], x1[:, slot + u, HALF:P], start=True, stop=False)
                    last = PE.matmul(dst, shift[:, 1, :], x1[:, slot + u - 1, HALF:P], start=False, stop=True)
                last.then_inc(m_sh, 1)
                pe.wait_ge(m_n, START + g + 1)
                for u in range(GROUP):
                    last = PE.transpose(ps[3][:, u * P:(u + 1) * P], h2n[:, u, :], ident[:, :])
                last.then_inc(m_T, 1)
                pe.wait_ge(m_Ts, START + g + 1)
                pe.wait_ge(s_w1, l * 16 + 16)
                for c in range(CH):
                    rows = P if c < CH - 1 else TAIL
                    for k in range(2):
                        PE.matmul(ps[c][0:rows, k * 512:(k + 1) * 512], w1_sb[:, k * HID + c * P:k * HID + c * P + rows],
                                  h2T[:, :], **one).then_inc(m_u, 1)
                pe.wait_ge(m_h, START + g * CH + CH)
                for u in range(GROUP):
                    for c in range(CH):
                        rows = P if c < CH - 1 else TAIL + 1
                        last = PE.matmul(ps[3][:, u * P:(u + 1) * P], gT[0:rows, c, u * P:(u + 1) * P],
                                         w2_sb[0:rows, l, c, :], start=(c == 0), stop=(c == CH - 1))
                last.then_inc(m_d, 1)

    return nc


def kernel(**inputs):
    import ml_dtypes
    import numpy as np
    import concourse.bacc as bacc
    from concourse.bass_utils import run_bass_kernel_spmd

    nc = bacc.Bacc("TRN2", target_bir_lowering=False, num_devices=1)
    names = ["L0_attn_x", "L0_attn_norm_g", "L0_attn_Wq", "L0_attn_Wkv", "L0_attn_Wout", "L0_attn_out_norm_g",
             "L0_ffn_wqkv", "L0_ffn_q_scale", "L0_ffn_k_scale", "L0_ffn_wo", "L0_ffn_ln_g", "L0_ffn_ln_b",
             "L0_ffn_w1", "L0_ffn_b1", "L0_ffn_w2", "L0_ffn_b2"]
    arrays = {name: np.ascontiguousarray(inputs[name]) for name in names}
    for name in ("L0_ffn_ln_g", "L0_ffn_ln_b"):
        arrays[name] = np.ascontiguousarray(arrays[name].T)
    B, N, D = arrays["L0_attn_x"].shape
    DH, WINDOW, P = arrays["L0_ffn_q_scale"].shape[1], 64, 128
    f4 = np.float32
    half_idx = np.arange(0, DH, 2, dtype=f4)
    inv_freq = (f4(1.0) / f4(10000.0) ** (half_idx / f4(DH))).astype(f4)
    t = np.arange(N, dtype=f4)
    freqs = (t[:, None] * inv_freq[None, :]).astype(f4)
    base = ((half_idx + f4(0.4 * DH)) / f4(1.4 * DH)).astype(f4)
    scale = (base[None, :] ** ((t - N // 2) / f4(WINDOW // 2))[:, None]).astype(f4)
    cos, sin = np.cos(freqs), np.sin(freqs)
    both = lambda a, b: np.concatenate([a, b], axis=1).astype(f4)
    qs, ks = 8 * scale, 1 / scale
    arrays["rope"] = np.stack([both(cos * qs, cos * qs), both(cos * ks, cos * ks),
                               both(-sin * qs, sin * qs), both(-sin * ks, sin * ks)])
    arrays["ident"] = np.eye(P, dtype=f4)
    arrays["identh"] = np.eye(P, dtype=np.float16)
    first = np.zeros((P, P), f4)
    first[P - 1, 0] = 1
    arrays["shift"] = np.stack([np.eye(P, k=1, dtype=f4), first])
    i, j = np.arange(P)[:, None], np.arange(P)[None, :]
    low = i < WINDOW
    own = np.where(low, (j < WINDOW) & (j <= i), (j <= i) & (i - j <= WINDOW))
    prev = low & (j >= WINDOW) & (j >= i + WINDOW)
    arrays["mask"] = np.stack([np.eye(P), np.where(own, 0, -1e38), np.where(own | prev, 0, -1e38)])\
        .astype(ml_dtypes.bfloat16)
    arrays["keep"] = np.stack([np.ones(P), np.zeros(P)], axis=1).astype(f4)
    args = [nc.dram_tensor("in_" + k, v.shape, mybir.dt.from_np(v.dtype), kind="ExternalInput").ap()
            for k, v in arrays.items()]
    out = nc.dram_tensor("out", (B, N, D), mybir.dt.float32, kind="ExternalOutput").ap()
    gated_mqa_local_block(nc, *args, out)
    r = run_bass_kernel_spmd(nc, [{"in_" + k: v for k, v in arrays.items()}], core_ids=[0])
    return r.results[0]["out"]
```

```python
import concourse.bass as bass
from concourse import mybir
from contextlib import ExitStack

import numpy as np


def gated_mqa_local_block(nc, x, norm_g, wq, wkv, wout, out_norm_g, wqkv, q_scale, k_scale, wo, ln_g, ln_b,
                          w1, b1, w2, b2, rope, ident_in, identh_in, shift_in, mask_in, keep_in, out):
    f32, f32r, f16, bf16 = mybir.dt.float32, mybir.dt.float32r, mybir.dt.float16, mybir.dt.bfloat16
    ALU, ACT, AX = mybir.AluOpType, mybir.ActivationFunctionType, mybir.AxisListType

    P = 128
    B, N, DIM = x.shape
    TILES = B * N // P
    TB = N // P
    DEPTH, _, QKV = wqkv.shape
    INNER = QKV // 3
    DH = q_scale.shape[1]
    HEADS = INNER // DH
    PAIRS = HEADS // 2
    HID = w2.shape[1]
    CH = -(-HID // P)
    TAIL = HID - (CH - 1) * P
    GROUP = 4
    HALF = P // 2
    HV = DH + 1
    VW = 2 * DH + 2
    EPS = 1e-5
    TINY = 1e-24
    QS = 64.0
    GROUPS = DEPTH * TILES // GROUP
    MICRO = 512
    CPU = TB // 2
    CPT = PAIRS * CPU
    CPG = TILES * CPT // GROUPS
    AHEAD = 3
    RING = 4
    ATT_SCALE = 16.0 / (QS * QS)

    with ExitStack() as ctx:
        def sb(name, shape, dt=f32):
            return ctx.enter_context(nc.sbuf_tensor(name, shape, dt))

        def sem(name):
            return ctx.enter_context(nc.semaphore(name))

        wq_sb = sb("wq_sb", [P, INNER])
        wkv_sb = sb("wkv_sb", [P, 2 * DH])
        wout_sb = sb("wout_sb", [P, PAIRS, DIM])
        wqkv_sb = sb("wqkv_sb", [P, DEPTH, QKV])
        wo_sb = sb("wo_sb", [P, DEPTH, PAIRS, DIM])
        w1_sb = sb("w1_sb", [P, 2 * HID])
        w2_sb = sb("w2_sb", [P, DEPTH, CH, DIM])
        b1_sb = sb("b1_sb", [P, DEPTH, 2, CH])
        lng_sb = sb("lng_sb", [P, DEPTH])
        lnb_sb = sb("lnb_sb", [P, DEPTH])
        ng_sb = sb("ng_sb", [P, 1])
        og_sb = sb("og_sb", [P, DIM])
        qk_scale = sb("qk_scale", [P, DEPTH, 4, DH])
        table = sb("table", [P, DEPTH, TB, 4, DH])
        ident = sb("ident", [P, P])
        shift = sb("shift", [P, 2, P])
        identb = sb("identb", [P, P], bf16)
        identh = sb("identh", [P, P], f16)
        mask = sb("mask", [P, TB, P], bf16)
        keep = sb("keep", [P, 2])
        neg_half = sb("neg_half", [P, 2 * HEADS])
        xs = sb("xs", [P, TILES, DIM])
        xnn = sb("xnn", [P, TILES, DIM])
        bn = sb("bn", [P, TILES, 6])
        mean = sb("mean", [P, TILES])
        scr = sb("scr", [P, 3, TILES])
        var = sb("var", [P, TILES])
        rstd = sb("rstd", [P, TILES])
        qT16 = sb("qT16", [P, TILES, HEADS, P], f16)
        late = qT16[:, :, :, :].rearrange("p t h n -> p (t h n)").bitcast(f32)
        x_in = late[:, 0:TILES * DIM].rearrange("p (t d) -> p t d", d=DIM)
        e_silu = late[:, TILES * DIM:2 * TILES * DIM]
        kT16 = sb("kT16", [P, TILES, 2, P], f16)
        v_r = sb("v_r", [P, TILES, VW], f32r)
        aT = sb("aT", [P, 2, P])
        xst = sb("xst", [P, 2, P])
        sq = sb("sq", [P, 2 * INNER])
        ss = sb("ss", [P, 2 * HEADS])
        rn = sb("rn", [P, 2 * HEADS])
        qn = sb("qn", [P, 2 * INNER])
        q16 = sb("q16", [P, 2, HEADS, 2, DH], f16)
        k16 = sb("k16", [P, 2, 2, 2, DH], f16)
        oa = sb("oa", [P, HEADS, DH])
        oaT = sb("oaT", [P, PAIRS, P])
        rden = sb("rden", [P, HEADS])
        p32 = sb("p32", [P, RING, MICRO])
        p_hi = sb("p_hi", [P, RING, MICRO], f32r)
        p_lo = sb("p_lo", [P, RING, MICRO], f32r)
        rqk = sb("rqk", [P, 2 * INNER])
        x1 = sb("x1", [P, GROUP + 1, DIM])
        v_own = sb("v_own", [P, GROUP, HEADS, HV])
        v_mix = sb("v_mix", [P, GROUP, HEADS, HV])
        sc = sb("sc", [P, HEADS * P])
        pr = sc
        prT = q16[:, :, :, :, :].rearrange("p a h k d -> p (a h k d)").bitcast(f32)\
            .rearrange("p (h n) -> p h n", n=P)
        o = sb("o", [P, INNER])
        oT = sb("oT", [P, PAIRS, P])
        h2 = sb("h2", [P, GROUP, DIM])
        h2T = sb("h2T", [P, GROUP * P])
        gT = sb("gT", [P, CH, GROUP * P])
        hT = sb("hT", [P, 2, P + 1])
        rot = sq
        qT = sb("qT", [P, PAIRS, P])
        kT = sb("kT", [P, 2, PAIRS, P])
        mx = sb("mx", [P, HEADS])
        o_dummy = sb("o_dummy", [P, 1])
        frd = sb("frd", [P, HEADS])
        fbn = sb("fbn", [P, GROUP, 6])
        fmean = sb("fmean", [P, GROUP])
        fscr = sb("fscr", [P, 3, GROUP])
        fvar = sb("fvar", [P, GROUP])
        frs = sb("frs", [P, GROUP])


        psX = ctx.enter_context(nc.psum_tensor("psX", [P, 1024], f32))
        psY = ctx.enter_context(nc.psum_tensor("psY", [P, 1024], f32))
        psZ = ctx.enter_context(nc.psum_tensor("psZ", [P, 512], f32))
        psS = ctx.enter_context(nc.psum_tensor("psS", [P, 2, MICRO], f32))
        psV = ctx.enter_context(nc.psum_tensor("psV", [P, 512], f32))
        head_of = [psX, psY]
        psS16 = psS[:, :, :].rearrange("p a b -> p (a b)")

        s_w = sem("s_w")
        s_x = sem("s_x")
        s_w1 = sem("s_w1")
        s_out = sem("s_out")
        dch = sem("dch")
        s_init = sem("s_init")
        s_pow = sem("s_pow")
        s_pq = sem("s_pq")
        s_tab = sem("s_tab")
        a_st = sem("a_st")
        a_T = sem("a_T")
        a_Ts = sem("a_Ts")
        n_done = sem("n_done")
        a_proj = sem("a_proj")
        a_sq = sem("a_sq")
        a_split = sem("a_split")
        a_tr = sem("a_tr")
        a_trs = sem("a_trs")
        a_qk = sem("a_qk")
        a_exp = sem("a_exp")
        a_hl = sem("a_hl")
        a_pv = sem("a_pv")
        a_or = sem("a_or")
        a_o = sem("a_o")
        a_oT = sem("a_oT")
        a_oTs = sem("a_oTs")
        a_wo = sem("a_wo")
        a_lin = sem("a_lin")
        f_st = sem("f_st")
        f_xT = sem("f_xT")
        f_hT = sem("f_hT")
        f_proj = sem("f_proj")
        f_sq = sem("f_sq")
        f_v = sem("f_v")
        f_n = sem("f_n")
        f_c = sem("f_c")
        f_cos = sem("f_cos")
        f_rope = sem("f_rope")
        f_tr = sem("f_tr")
        f_trs = sem("f_trs")
        f_s = sem("f_s")
        f_sub = sem("f_sub")
        f_exp = sem("f_exp")
        f_pT = sem("f_pT")
        f_pTs = sem("f_pTs")
        f_pv = sem("f_pv")
        f_o = sem("f_o")
        f_oT = sem("f_oT")
        f_oTs = sem("f_oTs")
        f_wo = sem("f_wo")
        f_x1 = sem("f_x1")
        m_sh = sem("m_sh")
        m_n = sem("m_n")
        m_T = sem("m_T")
        m_Ts = sem("m_Ts")
        m_u = sem("m_u")
        m_g = sem("m_g")
        m_h = sem("m_h")
        m_d = sem("m_d")
        m_x = sem("m_x")
        e_e = sem("e_e")

        START = RING
        counters = [a_T, a_Ts, a_exp, a_hl, a_lin, a_o, a_oT, a_oTs, a_or, a_proj, a_pv, a_qk, a_split,
                    a_sq, a_st, a_tr, a_trs, a_wo, f_c, f_cos, f_exp, f_hT, f_n, f_o, f_oT, f_oTs, f_pT, f_pTs, f_proj, f_pv,
                    f_rope, f_s, f_sq, f_st, f_sub, f_tr, f_trs, f_v, f_wo, f_x1, f_xT, m_T, m_Ts, m_d, m_g, m_h, m_n, m_sh, m_u, m_x]

        block = ctx.enter_context(nc.Block())

        N_W = 16 * (16 + DEPTH * (13 + 2 * CH))

        NEXT = ("stage", "load", "lanes", "project", "square", "lengths", "root", "norm", "cosine", "sine", "rotate", "keep")
        STEP = """stage T load copyqk scores lanes maximum micro exp project square probs copyprobs lengths micro
                 keep values average root norm micro sine micro cosine turn copyo output rotate residual micro
                 micro""".split()
        LAST_STEP = """micro turnA0 copyA0 micro outputA0 statsA0 T stage load lanes copyqk micro micro micro scores
                 maximum micro project exp square lengths probs copyprobs micro keep values average micro root
                 turn norm copyo micro output residual micro shift mstats micro sine mroot micro mnorm micro
                 micro turnh copyh up0 gelu0 up1 gate0 gelu1 cosine rotate gate1 up2 gelu2 gate2 turnA1 copyA1
                 down outputA1 store statsA1""".split()

        def group_events(last):
            m = 0
            for u in range(GROUP):
                for kind in (LAST_STEP if u == GROUP - 1 else STEP):
                    if kind == "micro":
                        yield kind, m
                        m += 1
                    elif kind in NEXT:
                        if not last or u + 1 < GROUP:
                            yield kind, u + 1
                    elif kind[-1] in "012":
                        yield kind[:-1], int(kind[-1])
                    else:
                        yield kind, u
            assert m == CPG

        def run(eng, do, prologue):
            prologue()
            with eng.Fori(0, GROUPS - 1) as g:
                for kind, u in group_events(False):
                    do(kind, u, g, False)
            for kind, u in group_events(True):
                do(kind, u, GROUPS - 1, True)

        def place(g, u):
            if u == GROUP:
                g, u = g + 1, 0
            r = g % (TILES // GROUP)
            return g * GROUP + u, g // (TILES // GROUP), r * GROUP + u, (g % (TB // GROUP)) * GROUP + u

        def micro_place(g, m):
            tile = m // CPT
            return g * CPG + m, g * (CPG // CPT) + tile, ((g * (CPG // CPT) + tile) // TB) * TB, m // CPU % PAIRS, m % CPU

        @block.sync
        def _(sp):
            for counter in counters:
                sp.sem_inc(counter, START)
            for c in range(4):
                t = TILES // 4
                b, o0 = divmod(c * t, TB)
                sp.dma_start(x_in[:, c * t:(c + 1) * t, :],
                             x[b, o0 * P:(o0 + t) * P, :].rearrange("(t p) d -> p t d", p=P)).then_inc(s_x, 16)
            loads = [
                (ident[:, :], ident_in), (ng_sb[:, :], norm_g.rearrange("(p o) -> p o", o=1)),
                (wq_sb[:, :], wq), (wkv_sb[:, :], wkv),
                (identb[:, :], mask_in[0]), (identh[:, :], identh_in),
                (wout_sb[:, :, :], wout.rearrange("(c p) n -> p c n", p=P)),
                (og_sb[:, :], out_norm_g.rearrange("(o d) -> o d", o=1).to_broadcast([P, DIM])),
                (wqkv_sb[:, :, :], wqkv.rearrange("l p n -> p l n")),
                (wo_sb[:, :, :, :], wo.rearrange("l (c p) n -> p l c n", p=P)),
                (mask[:, 0:1, :], mask_in[1:2].rearrange("t p n -> p t n")),
                (mask[:, 1:TB, :], mask_in[2:3].rearrange("t p n -> p t n").to_broadcast([P, TB - 1, P])),
                (shift[:, :, :], shift_in.rearrange("t p n -> p t n")),
                (keep[:, :], keep_in),
                (lng_sb[:, :], ln_g), (lnb_sb[:, :], ln_b),
            ]
            for l in range(DEPTH):
                loads += [(table[:, l, :, f, :], rope[f].rearrange("(t p) d -> p t d", p=P)) for f in range(4)]
                loads += [
                    (w2_sb[:, l, 0:CH - 1, :], w2[l, 0:(CH - 1) * P, :].rearrange("(c p) n -> p c n", p=P)),
                    (w2_sb[0:TAIL, l, CH - 1, :], w2[l, (CH - 1) * P:HID, :]),
                    (w2_sb[TAIL:TAIL + 1, l, CH - 1, :], b2[l:l + 1, :]),
                ]
                for k, v in ((0, q_scale), (1, k_scale)):
                    row = v[l:l + 1, :]
                    loads += [(qk_scale[:, l, k, :], row.to_broadcast([P, DH])),
                              (qk_scale[:, l, 2 + k, 0:DH // 2], row[:, DH // 2:DH].to_broadcast([P, DH // 2])),
                              (qk_scale[:, l, 2 + k, DH // 2:DH], row[:, 0:DH // 2].to_broadcast([P, DH // 2]))]
                for k in range(2):
                    for c in range(CH):
                        rows = P if c < CH - 1 else TAIL
                        at0 = k * HID + c * P
                        loads += [(b1_sb[0:rows, l, k, c:c + 1],
                                   b1[l, at0:at0 + rows].rearrange("(p o) -> p o", o=1))]
            assert 16 * len(loads) == N_W
            for dst, src in loads:
                sp.dma_start(dst, src).then_inc(s_w, 16)
            with sp.Fori(0, DEPTH) as l:
                sp.wait_ge(m_u, START + l * (TILES // GROUP) * 2 * CH)
                sp.dma_start(w1_sb[:, :], w1[l]).then_inc(s_w1, 16)
            sp.wait_ge(a_qk, START + GROUPS * CPG)
            for c in range(4):
                t = TILES // 4
                b, o0 = divmod(c * t, TB)
                sp.dma_start(x_in[:, c * t:(c + 1) * t, :],
                             x[b, o0 * P:(o0 + t) * P, :].rearrange("(t p) d -> p t d", p=P)).then_inc(s_x, 16)
            sp.wait_ge(e_e, 2)
            for c in range(4):
                t = TILES // 4
                b, o0 = divmod(c * t, TB)
                sp.dma_start(out[b, o0 * P:(o0 + t) * P, :].rearrange("(t p) d -> p t d", p=P),
                             xs[:, c * t:(c + 1) * t, :]).then_inc(s_out, 16)
            sp.wait_ge(s_out, 64)

        @block.gpsimd
        def _(pool):
            pool.memset(neg_half[:, :], -0.5)
            pool.memset(x1[:, 0, :], 0.0)
            pool.memset(v_own[:, :, :, DH:HV], 1.0)
            pool.memset(v_mix[:, :, :, DH:HV], 1.0)
            pool.memset(v_mix[:, 0, :, 0:DH], 0.0)
            pool.memset(gT[:, CH - 1, :], 1.0)
            pool.memset(hT[:, :, :], 0.0)
            pool.memset(kT[:, :, :, :], 0.0)
            pool.memset(qn[:, 0:16 * 2], 0.0)
            pool.memset(p32[:, 0, 0:TILES], 1.0)
            pool.memset(p32[:, 0, TILES:2 * TILES], 0.0).then_inc(s_init, 1)
            for k in range(2):
                pool.wait_ge(s_pq, k + 1)
                pool.tensor_tensor(rstd[:, :], var[:, :], neg_half[:, 0:TILES], ALU.pow).then_inc(s_pow, 1)
            pool.wait_ge(s_w, N_W)
            for l in range(DEPTH):
                for f in range(4):
                    last = pool.tensor_tensor(table[:, l, :, f, :], table[:, l, :, f, :],
                                              qk_scale[:, l, f:f + 1, :].to_broadcast([P, TB, DH]), ALU.mult)
            last.then_inc(s_tab, 1)
            with pool.Fori(0, TILES) as t:
                pool.wait_ge(s_pq, t + 3)
                pool.tensor_tensor(rn[:, 0:HEADS + 1], ss[:, 0:HEADS + 1], neg_half[:, 0:HEADS + 1],
                                   ALU.pow).then_inc(s_pow, 1)
            R0 = TILES + 2

            def pow_tile(u, g):
                n, _, _, _ = place(g, u)
                extra = g + 1 if u == GROUP else g
                if u == GROUP:
                    extra = g
                return R0 + n + extra + 1

            def do(kind, u, g, last):
                if kind == "root":
                    pool.wait_ge(s_pq, pow_tile(u, g))
                    pool.tensor_tensor(rn[:, :], ss[:, :], neg_half[:, :], ALU.pow).then_inc(s_pow, 1)
                elif kind == "sine":
                    n, l, _, t = place(g, u)
                    pool.wait_ge(f_n, START + n + 1)
                    src = qn[:, :].rearrange("p (k h d) -> p k h d", k=2, d=DH)
                    dst = rot[:, :].rearrange("p (k h d) -> p k h d", k=2, d=DH)
                    hd = DH // 2
                    for k in range(2):
                        for a, c in ((0, hd), (hd, 0)):
                            last_ = pool.tensor_tensor(
                                dst[:, k, :, a:a + hd], src[:, k, :, c:c + hd],
                                table[:, l, t, 2 + k:3 + k, a:a + hd].to_broadcast([P, HEADS, hd]), ALU.mult)
                    last_.then_inc(f_c, 1)
                elif kind == "mroot":
                    ready = g * (GROUP + 1) + GROUP + (1 if last else 2)
                    pool.wait_ge(s_pq, R0 + ready)
                    pool.tensor_tensor(frs[:, :], fvar[:, :], neg_half[:, 0:GROUP], ALU.pow).then_inc(s_pow, 1)

            def prologue():
                do("root", 0, 0, False)
                do("sine", 0, 0, False)

            run(pool, do, prologue)
            ROOTS = R0 + GROUPS * (GROUP + 1)
            pool.wait_ge(s_pq, ROOTS + 1)
            pool.tensor_tensor(rstd[:, :], var[:, :], neg_half[:, 0:TILES], ALU.pow).then_inc(s_pow, 1)

        @block.scalar
        def _(act):
            act.wait_ge(s_w, N_W)

            def front(t, u):
                act.wait_ge(a_T, START + t)
                act.wait_ge(n_done, 1)
                act.activation(xst[:, u, :], xnn[:, t, :], ACT.Copy).then_inc(a_st, 1)
                act.wait_ge(a_T, START + t + 1)
                act.activation(aT[:, u, :], psZ[:, 0:P], ACT.Copy, scale=ng_sb[:, 0:1]).then_inc(a_Ts, 1)
                act.wait_ge(a_proj, START + t + 1)
                act.wait_ge(s_pq, t + 2)
                act.activation(sq[:, 0:INNER + DH], head_of[u][:, 0:INNER + DH], ACT.Square).then_inc(a_sq, 1)

            def back(t, u):
                act.wait_ge(a_tr, START + t + 1)
                act.activation(qT16[:, t, :, :], psS[:, 0, :].bitcast(f16), ACT.Copy)
                act.activation(kT16[:, t, :, :], psS[:, 1, 0:P].bitcast(f16), ACT.Copy).then_inc(a_trs, 1)

            front(0, 0)
            with act.Fori(0, TILES // 2 - 1) as i:
                front(i * 2 + 1, 1)
                back(i * 2, 0)
                front(i * 2 + 2, 0)
                back(i * 2 + 1, 1)
            front(TILES - 1, 1)
            back(TILES - 2, 0)
            back(TILES - 1, 1)

            def do(kind, u, g, last):
                if kind == "micro":
                    if last and u + AHEAD >= CPG:
                        return
                    m, _, _, _, _ = micro_place(g, u + AHEAD)
                    exponentials(m, u + AHEAD)
                    return
                n, l, tile, _ = place(g, u)
                if kind == "stage":
                    load(n, tile, g, u)
                elif kind == "square":
                    act.wait_ge(f_proj, START + n + 1)
                    act.wait_ge(f_rope, START + n)
                    act.activation(sq[:, :], psX[:, :], ACT.Square).then_inc(f_sq, 1)
                elif kind == "keep":
                    src = psZ[:, 0:INNER].rearrange("p (h d) -> p h d", d=DH)
                    act.wait_ge(f_pv, START + n - 2)
                    act.activation(v_own[:, u % GROUP, :, 0:DH], src, ACT.Copy)
                    act.activation(v_mix[0:HALF, u % GROUP, :, 0:DH], src[0:HALF], ACT.Copy)
                    act.activation(v_mix[HALF:P, (u + 1) % GROUP, :, 0:DH], src[HALF:P], ACT.Copy).then_inc(f_v, 1)
                elif kind == "copyqk":
                    act.wait_ge(f_tr, START + n + 1)
                    act.wait_ge(f_s, START + n)
                    act.activation(qT[:, :, :], psY[:, 0:512], ACT.Copy)
                    act.activation(kT[:, u % 2, :, :], psY[:, 512:1024], ACT.Copy).then_inc(f_trs, 1)
                elif kind == "exp":
                    act.wait_ge(f_sub, START + n + 1)
                    act.wait_ge(f_pT, START + n)
                    act.activation(pr[:, :], sc[:, :], ACT.Exp).then_inc(f_exp, 1)
                elif kind == "copyprobs":
                    act.wait_ge(f_pT, START + n + 1)
                    act.wait_ge(f_pv, START + n)
                    act.activation(prT[:, :, :], psY[:, :], ACT.Copy).then_inc(f_pTs, 1)
                elif kind == "copyo":
                    act.wait_ge(f_oT, START + n + 1)
                    act.wait_ge(f_wo, START + n)
                    act.activation(oT[:, :, :], psZ[:, 0:512], ACT.Copy).then_inc(f_oTs, 1)
                elif kind == "copyh":
                    act.wait_ge(m_T, START + g + 1)
                    act.activation(h2T[:, :], psZ[:, 0:512], ACT.Identity, scale=lng_sb[:, bass.ds(l, 1)],
                                   bias=lnb_sb[:, bass.ds(l, 1)]).then_inc(m_Ts, 1)
                elif kind == "gelu":
                    c = u
                    _, l, _, _ = place(g, 0)
                    rows = P if c < CH - 1 else TAIL
                    act.wait_ge(m_u, START + g * 2 * CH + 2 * c + 2)
                    act.wait_ge(m_d, START + g)
                    act.activation(gT[0:rows, c, :], (psX, psY)[c % 2][0:rows, 512:1024], ACT.Gelu,
                                   bias=b1_sb[0:rows, l, 1, c:c + 1]).then_inc(m_g, 1)
                elif kind == "copyA":
                    t = g * (CPG // CPT) + u
                    act.wait_ge(a_oT, START + t + 1)
                    act.activation(oaT[:, :, :], psY[:, 0:512], ACT.Copy).then_inc(a_oTs, 1)

            def exponentials(m, j):
                act.wait_ge(a_qk, START + m + 1)
                act.wait_ge(a_pv, START + m - RING + 1)
                act.activation(p32[:, j % RING, :], psS[:, j % 2, :], ACT.Exp, scale=ATT_SCALE)
                act.activation(p_hi[:, j % RING, :], psS[:, j % 2, :], ACT.Exp, scale=ATT_SCALE).then_inc(a_exp, 1)

            def load(n, tile, g, u):
                act.wait_ge(m_x, START + g)
                act.wait_ge(f_xT, START + n - 1)
                act.activation(xst[:, u % 2, :], xs[:, tile, :], ACT.Copy).then_inc(f_st, 1)

            def prologue():
                load(0, 0, 0, 0)
                do("square", 0, 0, False)
                do("keep", 0, 0, False)
                for m in range(AHEAD):
                    exponentials(m, m)

            run(act, do, prologue)
            act.wait_ge(m_x, START + GROUPS)
            act.wait_ge(a_qk, START + GROUPS * CPG)
            act.activation(e_silu, xs[:, :, :].rearrange("p t d -> p (t d)"),
                           ACT.Exp, scale=-1.0).then_inc(e_e, 1)

        @block.vector
        def _(dve):
            DVE = nc.vector

            class Chain:
                base = 0
                n = 0

            ch = Chain()

            def link(ins):
                ch.n += 1
                ins.then_inc(dch, 1)
                dve.wait_ge(dch, ch.base + ch.n)

            def statistics(stats, mean, variance, scratch):
                m0, m1, q0, q1 = (stats[:, :, c] for c in (1, 4, 2, 5))
                d, d2, m2 = (scratch[:, c, :] for c in range(3))
                DVE.tensor_tensor(mean, m0, m1, ALU.add)
                DVE.tensor_tensor(d, m0, m1, ALU.subtract)
                link(DVE.tensor_tensor(m2, q0, q1, ALU.add))
                DVE.tensor_scalar(mean, mean, 0.5, None, ALU.mult)
                DVE.tensor_scalar(m2, m2, 1.0 / DIM, EPS, ALU.mult, ALU.add)
                link(DVE.scalar_tensor_tensor(d2, d, 0.25, d, ALU.mult, ALU.mult))
                return DVE.tensor_tensor(variance, m2, d2, ALU.add)

            def norm(dst, src, k):
                if k == 0:
                    dve.wait_ge(s_x, 64)
                with dve.Fori(0, TILES) as t:
                    DVE.bn_stats(bn[:, t, :], src[:, t, :]).then_inc(dch, 1)
                ch.base = ch.base + TILES
                dve.wait_ge(dch, ch.base + ch.n)
                statistics(bn, mean[:, :], var[:, :], scr).then_inc(s_pq, 1)
                dve.wait_ge(s_pow, k + 1)
                with dve.Fori(0, TILES) as t:
                    DVE.tensor_scalar(dst[:, t, :], src[:, t, :], mean[:, bass.ds(t, 1)], rstd[:, bass.ds(t, 1)],
                                      ALU.subtract, ALU.mult).then_inc(dch, 1)
                ch.base = ch.base + TILES
                dve.wait_ge(dch, ch.base + ch.n)

            dve.wait_ge(s_init, 1)
            DVE.tensor_copy(v_r[:, :, 2 * DH:VW - 1], p32[:, 0, 0:TILES].unsqueeze(2))
            DVE.tensor_copy(v_r[:, :, VW - 1:VW], p32[:, 0, TILES:2 * TILES].unsqueeze(2)).then_inc(a_split, 1)
            norm(xs, x_in, 0)
            norm(xnn, xs, 1)
            DVE.memset(mx[:, 0:1], 0.0).then_inc(n_done, 1)
            ch.base, ch.n = ch.base + ch.n, 0
            A_STEPS = 6
            with dve.Fori(0, TILES // 2) as i:
                base0 = ch.base
                for u in range(2):
                    t = i * 2 + u
                    base = base0 + i * 2 * A_STEPS + u * A_STEPS
                    dve.wait_ge(a_sq, START + t + 1)
                    DVE.tensor_reduce(ss[:, 0:HEADS + 1], sq[:, 0:INNER + DH].rearrange("p (h d) -> p h d", d=DH),
                                      AX.X, ALU.add).then_inc(dch, 1)
                    dve.wait_ge(dch, base + 1)
                    DVE.tensor_scalar(ss[:, 0:HEADS + 1], ss[:, 0:HEADS + 1], TINY, None, ALU.max).then_inc(s_pq, 1)
                    dve.wait_ge(s_pow, t + 3)
                    DVE.tensor_scalar(rn[:, 0:HEADS + 1], rn[:, 0:HEADS + 1], QS, None, ALU.mult).then_inc(dch, 1)
                    dve.wait_ge(dch, base + 2)
                    q_ps = head_of[u][:, 0:INNER + DH].rearrange("p (h d) -> p h d", d=DH)
                    DVE.tensor_tensor(qn[:, 0:INNER + DH].rearrange("p (h d) -> p h d", d=DH), q_ps,
                                      rn[:, 0:HEADS + 1].unsqueeze(2).to_broadcast([P, HEADS + 1, DH]),
                                      ALU.mult).then_inc(dch, 1)
                    DVE.tensor_copy(v_r[:, t, 0:DH], head_of[u][:, INNER + DH:INNER + 2 * DH]).then_inc(dch, 1)
                    dve.wait_ge(dch, base + 4)
                    DVE.tensor_tensor(v_r[:, t, DH:2 * DH], head_of[u][:, INNER + DH:INNER + 2 * DH],
                                      v_r[:, t, 0:DH].bitcast(f32), ALU.subtract).then_inc(dch, 1)
                    dve.wait_ge(a_tr, START + i * 2)
                    qf = qn[:, 0:INNER].rearrange("p (h d) -> p h d", d=DH)
                    kf = qn[:, INNER:INNER + DH]
                    DVE.tensor_copy(q16[:, u, :, 0, :], qf)
                    DVE.tensor_copy(k16[:, u, 0, 0, :], kf)
                    DVE.tensor_copy(k16[:, u, 1, 1, :], kf).then_inc(dch, 1)
                    dve.wait_ge(dch, base + 6)
                    DVE.tensor_tensor(q16[:, u, :, 1, :], qf, q16[:, u, :, 0, :], ALU.subtract)
                    DVE.tensor_tensor(k16[:, u, 0, 1, :], kf, k16[:, u, 0, 0, :], ALU.subtract)
                    DVE.tensor_tensor(k16[:, u, 1, 0, :], kf, k16[:, u, 0, 0, :], ALU.subtract).then_inc(a_split, 1)
            ch.base = ch.base + TILES * A_STEPS

            R0 = TILES + 2
            dve.wait_ge(s_tab, 1)

            def heads(t, k=HEADS):
                return t.rearrange("p (h d) -> p h d", h=k)

            def split(m, j):
                dve.wait_ge(a_exp, START + m + 1)
                DVE.tensor_tensor(p_lo[:, j % RING, :], p32[:, j % RING, :], p_hi[:, j % RING, :].bitcast(f32),
                                  ALU.subtract).then_inc(a_hl, 1)

            def average(g, j):
                _, t, _, hp, _ = micro_place(g, j)
                unit = g * (CPG // CPU) + j // CPU
                dve.wait_ge(a_pv, START + (unit + 1) * CPU)
                if hp == 0:
                    dve.wait_ge(a_oT, START + t)
                pv = heads(psV[:, 0:2 * VW], 2)
                DVE.reciprocal(rden[:, 0:2], pv[:, :, 2 * DH])
                DVE.tensor_reduce(oa[:, 2 * hp:2 * hp + 2, :],
                                  pv[:, :, 0:2 * DH].rearrange("p h (a d) -> p h d a", a=2), AX.X,
                                  ALU.add).then_inc(a_or, 1)
                dve.wait_ge(a_or, START + unit + 1)
                DVE.tensor_tensor(oa[:, 2 * hp:2 * hp + 2, :], oa[:, 2 * hp:2 * hp + 2, :],
                                  rden[:, 0:2].unsqueeze(2).to_broadcast([P, 2, DH]), ALU.mult).then_inc(a_o, 1)

            def do(kind, u, g, last):
                if kind == "micro":
                    if not (last and u + AHEAD >= CPG):
                        m, _, _, _, _ = micro_place(g, u + AHEAD)
                        split(m, u + AHEAD)
                    if u % CPU == CPU - 1:
                        average(g, u)
                    return
                n, l, tile, t = place(g, u)
                if kind == "lanes":
                    dve.wait_ge(f_xT, START + n + 1)
                    dve.wait_ge(f_proj, START + n)
                    DVE.tensor_copy(hT[0:HALF, u % 2, 0:P], psZ[0:HALF, 0:P])
                    DVE.tensor_copy(hT[HALF:P, u % 2, 1:P + 1], psZ[HALF:P, 0:P])
                    nxt = hT[HALF:P, (u + 1) % 2, 0:1]
                    if u % GROUP < GROUP - 1:
                        DVE.tensor_copy(nxt, psZ[HALF:P, P - 1:P]).then_inc(f_hT, 1)
                    else:
                        DVE.tensor_scalar(nxt, psZ[HALF:P, P - 1:P], keep[HALF:P, bass.ds(g % (TB // GROUP), 1)],
                                          None, ALU.mult).then_inc(f_hT, 1)
                elif kind == "lengths":
                    dve.wait_ge(f_sq, START + n + 1)
                    link(DVE.tensor_reduce(ss[:, :], heads(sq[:, :], 2 * HEADS), AX.X, ALU.add))
                    DVE.tensor_scalar(ss[:, :], ss[:, :], TINY, None, ALU.max).then_inc(s_pq, 1)
                elif kind == "norm":
                    dve.wait_ge(s_pow, R0 + n + g + 1)
                    dve.wait_ge(f_c, START + n)
                    DVE.tensor_tensor(heads(qn[:, :], 2 * HEADS), heads(psX[:, :], 2 * HEADS),
                                      rn[:, :].unsqueeze(2).to_broadcast([P, 2 * HEADS, DH]),
                                      ALU.mult).then_inc(f_n, 1)
                elif kind == "cosine":
                    dve.wait_ge(f_n, START + n + 1)
                    dve.wait_ge(f_tr, START + n)
                    for k in range(2):
                        part = slice(k * INNER, (k + 1) * INNER)
                        last_ = DVE.tensor_tensor(heads(rqk[:, part]), heads(qn[:, part]),
                                                  table[:, l, t, k:k + 1, :].to_broadcast([P, HEADS, DH]), ALU.mult)
                    last_.then_inc(f_cos, 1)
                elif kind == "rotate":
                    dve.wait_ge(f_cos, START + n + 1)
                    dve.wait_ge(f_c, START + n + 1)
                    DVE.tensor_tensor(rqk[:, :], rqk[:, :], rot[:, :], ALU.add).then_inc(f_rope, 1)
                elif kind == "maximum":
                    dve.wait_ge(f_s, START + n + 1)
                    s3 = heads(psY[:, :])
                    link(DVE.tensor_reduce(mx[:, :], s3, AX.X, ALU.max))
                    dve.wait_ge(f_exp, START + n)
                    DVE.tensor_tensor(heads(sc[:, :]), s3, mx[:, :].unsqueeze(2).to_broadcast([P, HEADS, P]),
                                      ALU.subtract).then_inc(f_sub, 1)
                elif kind == "average":
                    dve.wait_ge(f_pv, START + n + 1)
                    pv = psY[:, :].rearrange("p (k n) -> p k n", k=2)[:, :, 0:PAIRS * HV]\
                        .rearrange("p k (h v) -> p k h v", v=HV)
                    link(DVE.reciprocal(frd[:, :].rearrange("p (k h) -> p k h", k=2), pv[:, :, :, DH]))
                    dve.wait_ge(f_oT, START + n)
                    for k in range(2):
                        last_ = DVE.tensor_tensor(
                            heads(o[:, k * INNER // 2:(k + 1) * INNER // 2], PAIRS), pv[:, k, :, 0:DH],
                            frd[:, k * PAIRS:(k + 1) * PAIRS].unsqueeze(2).to_broadcast([P, PAIRS, DH]), ALU.mult)
                    last_.then_inc(f_o, 1)
                elif kind == "residual":
                    dve.wait_ge(f_wo, START + n + 1)
                    DVE.tensor_tensor(x1[:, u + 1, :], psZ[:, 0:DIM], xs[:, tile, :], ALU.add).then_inc(f_x1, 1)
                elif kind == "mstats":
                    dve.wait_ge(m_sh, START + g + 1)
                    DVE.tensor_scalar(h2[:, :, 0:HALF], x1[:, 1:GROUP + 1, 0:HALF], 1.0, None, ALU.mult)
                    link(DVE.tensor_copy(h2[:, :, HALF:P], heads(psZ[:, 0:GROUP * HALF], GROUP)))
                    for i in range(GROUP):
                        last_ = DVE.bn_stats(fbn[:, i, :], h2[:, i, :])
                    link(last_)
                    statistics(fbn, fmean[:, :], fvar[:, :], fscr).then_inc(s_pq, 1)
                elif kind == "mnorm":
                    dve.wait_ge(s_pow, R0 + g * (GROUP + 1) + GROUP + (1 if last else 2))
                    for i in range(GROUP):
                        last_ = DVE.tensor_scalar(h2[:, i, :], h2[:, i, :], fmean[:, i:i + 1], frs[:, i:i + 1],
                                                  ALU.subtract, ALU.mult)
                    last_.then_inc(m_n, 1)
                elif kind == "gate":
                    c = u
                    _, l, _, _ = place(g, 0)
                    rows = P if c < CH - 1 else TAIL
                    dve.wait_ge(m_g, START + g * CH + c + 1)
                    DVE.scalar_tensor_tensor(gT[0:rows, c, :], (psX, psY)[c % 2][0:rows, 0:512],
                                             b1_sb[0:rows, l, 0, c:c + 1], gT[0:rows, c, :], ALU.add,
                                             ALU.mult).then_inc(m_h, 1)
                elif kind == "store":
                    tile = place(g, 0)[2]
                    dve.wait_ge(m_d, START + g + 1)
                    DVE.tensor_tensor(xs[:, bass.ds(tile, GROUP), :], x1[:, 1:GROUP + 1, :],
                                      heads(psZ[:, 0:GROUP * P], GROUP), ALU.add).then_inc(m_x, 1)
                    link(DVE.tensor_scalar(x1[:, 0, HALF:P], x1[:, GROUP, HALF:P],
                                           keep[:, bass.ds(g % (TB // GROUP), 1)], None, ALU.mult))
                elif kind == "statsA":
                    t = g * (CPG // CPT) + u
                    dve.wait_ge(a_wo, START + t + 1)
                    DVE.tensor_scalar(xnn[:, t, :], psY[:, 512:512 + DIM], 1.0, None, ALU.mult)
                    DVE.bn_stats(bn[:, t, :], psY[:, 512:512 + DIM]).then_inc(a_lin, 1)

            def prologue():
                for kind in ("lanes", "lengths", "norm", "cosine", "rotate"):
                    do(kind, 0, 0, False)
                for m in range(AHEAD):
                    split(m, m)

            GROUP_STEPS = 3 * GROUP + 5
            prologue()
            base0 = ch.base + ch.n
            with dve.Fori(0, GROUPS - 1) as g:
                ch.base, ch.n = base0 + g * GROUP_STEPS, 0
                for kind, u in group_events(False):
                    do(kind, u, g, False)
                assert ch.n == GROUP_STEPS, ch.n
            ch.base, ch.n = base0 + (GROUPS - 1) * GROUP_STEPS, 0
            for kind, u in group_events(True):
                do(kind, u, GROUPS - 1, True)
            dve.wait_ge(a_lin, START + TILES)
            ROOTS = R0 + GROUPS * (GROUP + 1)
            statistics(bn, mean[:, :], var[:, :], scr).then_inc(s_pq, 1)
            dve.wait_ge(s_pow, ROOTS + 1)
            with dve.Fori(0, TILES) as t:
                DVE.tensor_scalar(xnn[:, t, :], xnn[:, t, :], mean[:, bass.ds(t, 1)], rstd[:, bass.ds(t, 1)],
                                  ALU.subtract, ALU.mult).then_inc(dch, 1)
            ch.n += TILES
            dve.wait_ge(dch, ch.base + ch.n)
            link(DVE.tensor_tensor(xnn[:, :, :], xnn[:, :, :], og_sb[:, :].unsqueeze(1).to_broadcast([P, TILES, DIM]),
                                   ALU.mult))
            dve.wait_ge(e_e, 1)
            e = e_silu
            dve.wait_ge(s_x, 128)
            xf, sf, xi = (t[:, :, :].rearrange("p t d -> p (t d)") for t in (xs, xnn, x_in))
            link(DVE.tensor_scalar(e, e, 1.0, None, ALU.add))
            link(DVE.reciprocal(e, e))
            link(DVE.tensor_tensor(xf, xf, e, ALU.mult))
            link(DVE.tensor_tensor(xf, xf, sf, ALU.mult))
            DVE.tensor_tensor(xf, xf, xi, ALU.add).then_inc(e_e, 1)

        @block.tensor
        def _(pe):
            PE = nc.tensor
            one = dict(start=True, stop=True)
            pe.wait_ge(s_w, N_W)
            pe.wait_ge(n_done, 1)


            def front(t, u):
                pe.wait_ge(a_st, START + t + 1)
                pe.wait_ge(a_Ts, START + t)
                PE.transpose(psZ[:, 0:P], xst[:, u, :], ident[:, :]).then_inc(a_T, 1)
                pe.wait_ge(a_Ts, START + t + 1)
                pe.wait_ge(a_split, START + t)
                PE.matmul(head_of[u][:, 0:INNER], aT[:, u, :], wq_sb[:, :], **one)
                PE.matmul(head_of[u][:, INNER:INNER + 2 * DH], aT[:, u, :], wkv_sb[:, :], **one).then_inc(a_proj, 1)

            def back(t, u):
                pe.wait_ge(a_split, START + t + 2)
                pe.wait_ge(a_trs, START + t)
                for h in range(HEADS):
                    PE.transpose(psS[:, 0, h * HALF:(h + 1) * HALF].bitcast(f16),
                                 q16[:, u, h, :, :].rearrange("p a d -> p (a d)"), identh[:, :])
                for k in range(2):
                    last = PE.transpose(psS[:, 1, k * HALF:(k + 1) * HALF].bitcast(f16),
                                        k16[:, u, k, :, :].rearrange("p a d -> p (a d)"), identh[:, :])
                last.then_inc(a_tr, 1)

            front(0, 0)
            with pe.Fori(0, TILES // 2 - 1) as i:
                front(i * 2 + 1, 1)
                back(i * 2, 0)
                front(i * 2 + 2, 0)
                back(i * 2 + 1, 1)
            front(TILES - 1, 1)
            back(TILES - 2, 0)
            back(TILES - 1, 1)
            pe.wait_ge(a_trs, START + TILES)

            def queries(g, j):
                m, tile, kb, hp, c = micro_place(g, j)
                pe.wait_ge(a_exp, START + m - 1)
                for k in range(2):
                    for part in range(2):
                        last_ = PE.matmul(psS[:, j % 2, k * 256:(k + 1) * 256], kT16[:, kb + 2 * c + k, part, :],
                                          qT16[:, tile, 2 * hp:2 * hp + 2, :], start=(part == 0), stop=(part == 1))
                last_.then_inc(a_qk, 1)

            def values(g, j):
                m, _, kb, _, c = micro_place(g, j)
                if c == 0:
                    pe.wait_ge(a_o, START + g * (CPG // CPU) + j // CPU)
                pe.wait_ge(a_hl, START + m + 1)
                for k in range(2):
                    for pi, part in enumerate((p_hi, p_lo)):
                        for h in range(2):
                            last_ = PE.matmul(psV[:, h * VW:(h + 1) * VW],
                                              part[:, j % RING, k * 256 + h * P:k * 256 + (h + 1) * P],
                                              v_r[:, kb + 2 * c + k, :],
                                              start=(c == 0 and k == 0 and pi == 0 and h == 0),
                                              stop=(c == CPU - 1 and k == 1 and pi == 1), skip_group_check=True)
                last_.then_inc(a_pv, 1)

            def do(kind, u, g, last):
                if kind == "micro":
                    if not (last and u + AHEAD >= CPG):
                        queries(g, u + AHEAD)
                    values(g, u)
                    return
                n, l, _, t = place(g, u)
                if kind == "load":
                    pe.wait_ge(f_st, START + n + 1)
                    pe.wait_ge(f_x1, START + n - 1)
                    pe.wait_ge(m_x, START + g)
                    PE.transpose(psZ[:, 0:P], xst[:, u % 2, :], ident[:, :]).then_inc(f_xT, 1)
                elif kind == "project":
                    pe.wait_ge(f_hT, START + n + 1)
                    pe.wait_ge(f_n, START + n)
                    for k, dst in enumerate((psX[:, 0:512], psX[:, 512:1024], psZ[:, :])):
                        last_ = PE.matmul(dst, hT[:, u % 2, 0:P], wqkv_sb[:, l, k * INNER:(k + 1) * INNER], **one)
                    last_.then_inc(f_proj, 1)
                elif kind == "T":
                    pe.wait_ge(f_rope, START + n + 1)
                    pe.wait_ge(f_o, START + n)
                    pe.wait_ge(a_lin, START + g * (CPG // CPT) + (1 if u == GROUP - 1 else 0))
                    if u == 0:
                        pe.wait_ge(m_h, START + g * CH)
                    for k in range(2 * PAIRS):
                        last_ = PE.transpose(psY[:, k * P:(k + 1) * P], rqk[:, k * P:(k + 1) * P], ident[:, :])
                    last_.then_inc(f_tr, 1)
                elif kind == "scores":
                    pe.wait_ge(f_trs, START + n + 1)
                    for r in range(2):
                        PE.matmul(heads(psY[:, r * 512:(r + 1) * 512], PAIRS), identb[:, :],
                                  mask[:, bass.ds(t, 1), :].to_broadcast([P, PAIRS, P]),
                                  start=True, stop=False, skip_group_check=True)
                    rows = [slice(0, HALF), slice(HALF, P)]
                    cur, prev = u % 2, (u + 1) % 2
                    for k in range(PAIRS):
                        for r in range(2):
                            col = r * 512 + k * P
                            q, kc, kp = qT[rows[r], k, :], kT[rows[r], cur, k, :], kT[rows[r], prev, k, :]
                            acc = dict(start=False, stop=(k == PAIRS - 1), skip_group_check=True)
                            PE.matmul(psY[0:HALF, col:col + HALF], q[:, 0:HALF], kc[:, 0:HALF], **acc)
                            PE.matmul(psY[0:HALF, col + HALF:col + P], q[:, 0:HALF], kp[:, HALF:P], **acc)
                            last_ = PE.matmul(psY[HALF:P, col:col + P], q[:, HALF:P], kc, **acc)
                    last_.then_inc(f_s, 1)
                elif kind == "probs":
                    pe.wait_ge(f_exp, START + n + 1)
                    for k in range(HEADS):
                        last_ = PE.transpose(psY[:, k * P:(k + 1) * P], pr[:, k * P:(k + 1) * P], ident[:, :])
                    last_.then_inc(f_pT, 1)
                elif kind == "values":
                    pe.wait_ge(f_pTs, START + n + 1)
                    for h in range(HEADS):
                        at = (h % 2) * PAIRS + h // 2
                        col = (h // PAIRS) * 512 + (h % PAIRS) * HV
                        PE.matmul(psY[0:HALF, col:col + HV], prT[:, at, 0:HALF], v_mix[:, u, h, :], **one)
                        last_ = PE.matmul(psY[HALF:P, col:col + HV], prT[:, at, HALF:P], v_own[:, u, h, :], **one)
                    last_.then_inc(f_pv, 1)
                elif kind == "turn":
                    pe.wait_ge(f_o, START + n + 1)
                    pe.wait_ge(f_v, START + n + (1 if last and u == GROUP - 1 else 2))
                    for k in range(PAIRS):
                        last_ = PE.transpose(psZ[:, k * P:(k + 1) * P], o[:, k * P:(k + 1) * P], ident[:, :])
                    last_.then_inc(f_oT, 1)
                elif kind == "output":
                    pe.wait_ge(f_oTs, START + n + 1)
                    for k in range(PAIRS):
                        last_ = PE.matmul(psZ[:, 0:DIM], oT[:, k, :], wo_sb[:, l, k, :],
                                          start=(k == 0), stop=(k == PAIRS - 1))
                    last_.then_inc(f_wo, 1)
                elif kind == "shift":
                    pe.wait_ge(f_x1, START + g * GROUP + GROUP)
                    for i in range(GROUP):
                        dst = psZ[:, i * HALF:(i + 1) * HALF]
                        PE.matmul(dst, shift[:, 0, :], x1[:, i + 1, HALF:P], start=True, stop=False)
                        last_ = PE.matmul(dst, shift[:, 1, :], x1[:, i, HALF:P], start=False, stop=True)
                    last_.then_inc(m_sh, 1)
                elif kind == "turnh":
                    pe.wait_ge(m_n, START + g + 1)
                    for i in range(GROUP):
                        last_ = PE.transpose(psZ[:, i * P:(i + 1) * P], h2[:, i, :], ident[:, :])
                    last_.then_inc(m_T, 1)
                elif kind == "up":
                    c = u
                    _, l, _, _ = place(g, 0)
                    pe.wait_ge(m_Ts, START + g + 1)
                    pe.wait_ge(s_w1, l * 16 + 16)
                    pe.wait_ge(f_n, START + g * GROUP + GROUP + (0 if last else 1))
                    pe.wait_ge(f_o, START + g * GROUP + GROUP)
                    rows = P if c < CH - 1 else TAIL
                    if c >= 2:
                        pe.wait_ge(m_h, START + g * CH + c - 1)
                    for k in range(2):
                        PE.matmul((psX, psY)[c % 2][0:rows, k * 512:(k + 1) * 512],
                                  w1_sb[:, k * HID + c * P:k * HID + c * P + rows], h2T[:, :],
                                  **one).then_inc(m_u, 1)
                elif kind == "down":
                    pe.wait_ge(m_h, START + g * CH + CH)
                    for i in range(GROUP):
                        for c in range(CH):
                            rows = P if c < CH - 1 else TAIL + 1
                            last_ = PE.matmul(psZ[:, i * P:(i + 1) * P], gT[0:rows, c, i * P:(i + 1) * P],
                                              w2_sb[0:rows, l, c, :], start=(c == 0), stop=(c == CH - 1))
                    last_.then_inc(m_d, 1)
                elif kind == "turnA":
                    t = g * (CPG // CPT) + u
                    pe.wait_ge(a_o, START + (t + 1) * PAIRS)
                    if u == 0:
                        pe.wait_ge(f_o, START + g * GROUP + GROUP - 1)
                    else:
                        pe.wait_ge(m_h, START + g * CH + CH)
                    oflat = oa[:, :, :].rearrange("p h d -> p (h d)")
                    for k in range(PAIRS):
                        last_ = PE.transpose(psY[:, k * P:(k + 1) * P], oflat[:, k * P:(k + 1) * P], ident[:, :])
                    last_.then_inc(a_oT, 1)
                elif kind == "outputA":
                    t = g * (CPG // CPT) + u
                    pe.wait_ge(a_oTs, START + t + 1)
                    for k in range(PAIRS):
                        last_ = PE.matmul(psY[:, 512:512 + DIM], oaT[:, k, :], wout_sb[:, k, :],
                                          start=(k == 0), stop=(k == PAIRS - 1))
                    last_.then_inc(a_wo, 1)

            def heads(t, k):
                return t.rearrange("p (h d) -> p h d", h=k)

            def prologue():
                do("load", 0, 0, False)
                do("project", 0, 0, False)
                for m in range(AHEAD):
                    queries(0, m)

            run(pe, do, prologue)

    return nc


def kernel(**inputs):
    import ml_dtypes
    import numpy as np
    import concourse.bacc as bacc
    from concourse.bass_utils import run_bass_kernel_spmd

    nc = bacc.Bacc("TRN2", target_bir_lowering=False, num_devices=1)
    names = ["L0_attn_x", "L0_attn_norm_g", "L0_attn_Wq", "L0_attn_Wkv", "L0_attn_Wout", "L0_attn_out_norm_g",
             "L0_ffn_wqkv", "L0_ffn_q_scale", "L0_ffn_k_scale", "L0_ffn_wo", "L0_ffn_ln_g", "L0_ffn_ln_b",
             "L0_ffn_w1", "L0_ffn_b1", "L0_ffn_w2", "L0_ffn_b2"]
    arrays = {name: np.ascontiguousarray(inputs[name]) for name in names}
    for name in ("L0_ffn_ln_g", "L0_ffn_ln_b"):
        arrays[name] = np.ascontiguousarray(arrays[name].T)
    B, N, D = arrays["L0_attn_x"].shape
    DH, WINDOW, P = arrays["L0_ffn_q_scale"].shape[1], 64, 128
    f4 = np.float32
    half_idx = np.arange(0, DH, 2, dtype=f4)
    inv_freq = (f4(1.0) / f4(10000.0) ** (half_idx / f4(DH))).astype(f4)
    t = np.arange(N, dtype=f4)
    freqs = (t[:, None] * inv_freq[None, :]).astype(f4)
    base = ((half_idx + f4(0.4 * DH)) / f4(1.4 * DH)).astype(f4)
    scale = (base[None, :] ** ((t - N // 2) / f4(WINDOW // 2))[:, None]).astype(f4)
    cos, sin = np.cos(freqs), np.sin(freqs)
    both = lambda a, b: np.concatenate([a, b], axis=1).astype(f4)
    qs, ks = 8 * scale, 1 / scale
    arrays["rope"] = np.stack([both(cos * qs, cos * qs), both(cos * ks, cos * ks),
                               both(-sin * qs, sin * qs), both(-sin * ks, sin * ks)])
    arrays["ident"] = np.eye(P, dtype=f4)
    arrays["identh"] = np.eye(P, dtype=np.float16)
    first = np.zeros((P, P), f4)
    first[P - 1, 0] = 1
    arrays["shift"] = np.stack([np.eye(P, k=1, dtype=f4), first])
    i, j = np.arange(P)[:, None], np.arange(P)[None, :]
    low = i < WINDOW
    own = np.where(low, (j < WINDOW) & (j <= i), (j <= i) & (i - j <= WINDOW))
    prev = low & (j >= WINDOW) & (j >= i + WINDOW)
    arrays["mask"] = np.stack([np.eye(P), np.where(own, 0, -1e38), np.where(own | prev, 0, -1e38)])\
        .astype(ml_dtypes.bfloat16)
    arrays["keep"] = np.stack([np.ones(P), np.zeros(P)], axis=1).astype(f4)
    args = [nc.dram_tensor("in_" + k, v.shape, mybir.dt.from_np(v.dtype), kind="ExternalInput").ap()
            for k, v in arrays.items()]
    out = nc.dram_tensor("out", (B, N, D), mybir.dt.float32, kind="ExternalOutput").ap()
    gated_mqa_local_block(nc, *args, out)
    r = run_bass_kernel_spmd(nc, [{"in_" + k: v for k, v in arrays.items()}], core_ids=[0])
    return r.results[0]["out"]
```

```python
import concourse.bass as bass
from concourse import mybir
from contextlib import ExitStack

import numpy as np


def gated_mqa_local_block(nc, x, norm_g, wq, wkv, wout, out_norm_g, wqkv, q_scale, k_scale, wo, ln_g, ln_b,
                          w1, b1, w2, b2, rope, ident_in, identh_in, shift_in, mask_in, keep_in, out):
    f32, f32r, f16, bf16 = mybir.dt.float32, mybir.dt.float32r, mybir.dt.float16, mybir.dt.bfloat16
    ALU, ACT, AX = mybir.AluOpType, mybir.ActivationFunctionType, mybir.AxisListType

    P = 128
    B, N, DIM = x.shape
    TILES = B * N // P
    TB = N // P
    DEPTH, _, QKV = wqkv.shape
    INNER = QKV // 3
    DH = q_scale.shape[1]
    HEADS = INNER // DH
    PAIRS = HEADS // 2
    HID = w2.shape[1]
    CH = -(-HID // P)
    TAIL = HID - (CH - 1) * P
    GROUP = 4
    HALF = P // 2
    HV = DH + 1
    VW = 2 * DH + 2
    EPS = 1e-5
    TINY = 1e-24
    QS = 64.0
    GROUPS = DEPTH * TILES // GROUP
    MICRO = 512
    CPU = TB // 2
    CPT = PAIRS * CPU
    CPG = TILES * CPT // GROUPS
    AHEAD = 3
    SHIFT = 12
    RING = 4
    EARLY = TILES - GROUP
    ATT_SCALE = 16.0 / (QS * QS)

    with ExitStack() as ctx:
        def sb(name, shape, dt=f32):
            return ctx.enter_context(nc.sbuf_tensor(name, shape, dt))

        def sem(name):
            return ctx.enter_context(nc.semaphore(name))

        wq_sb = sb("wq_sb", [P, INNER])
        wkv_sb = sb("wkv_sb", [P, 2 * DH])
        wout_sb = sb("wout_sb", [P, PAIRS, DIM])
        wqkv_sb = sb("wqkv_sb", [P, DEPTH, QKV])
        wo_sb = sb("wo_sb", [P, DEPTH, PAIRS, DIM])
        w1_sb = sb("w1_sb", [P, 2 * HID])
        w2_sb = sb("w2_sb", [P, DEPTH, CH, DIM])
        b1_sb = sb("b1_sb", [P, DEPTH, 2, CH])
        lng_sb = sb("lng_sb", [P, DEPTH])
        lnb_sb = sb("lnb_sb", [P, DEPTH])
        ng_sb = sb("ng_sb", [P, 1])
        og_sb = sb("og_sb", [P, DIM])
        qk_scale = sb("qk_scale", [P, DEPTH, 4, DH])
        table = sb("table", [P, DEPTH, TB, 4, DH])
        ident = sb("ident", [P, P])
        shift = sb("shift", [P, 2, P])
        identb = sb("identb", [P, P], bf16)
        identh = sb("identh", [P, P], f16)
        mask = sb("mask", [P, TB, P], bf16)
        keep = sb("keep", [P, 2])
        neg_half = sb("neg_half", [P, 2 * HEADS])
        xs = sb("xs", [P, TILES, DIM])
        xnn = sb("xnn", [P, TILES, DIM])
        bn = sb("bn", [P, TILES, 6])
        mean = sb("mean", [P, TILES])
        scr = sb("scr", [P, 3, TILES])
        var = sb("var", [P, TILES])
        rstd = sb("rstd", [P, TILES])
        qT16 = sb("qT16", [P, TILES, HEADS, P], f16)
        late = qT16[:, :, :, :].rearrange("p t h n -> p (t h n)").bitcast(f32)
        x_in = late[:, 0:TILES * DIM].rearrange("p (t d) -> p t d", d=DIM)
        e_silu = late[:, TILES * DIM:2 * TILES * DIM]
        kT16 = sb("kT16", [P, TILES, 2, P], f16)
        v_r = sb("v_r", [P, TILES, VW], f32r)
        aT = sb("aT", [P, 2, P])
        xst = sb("xst", [P, 2, P])
        sq = sb("sq", [P, 2 * INNER])
        ss = sb("ss", [P, 2 * HEADS])
        rn = sb("rn", [P, 2 * HEADS])
        qn = sb("qn", [P, 2 * INNER])
        q16 = sb("q16", [P, 2, HEADS, 2, DH], f16)
        k16 = sb("k16", [P, 2, 2, 2, DH], f16)
        oa = sb("oa", [P, HEADS, DH])
        oaT = sb("oaT", [P, PAIRS, P])
        rden = sb("rden", [P, HEADS])
        a_ss = sb("a_ss", [P, 2, HEADS + 1])
        a_rn = sb("a_rn", [P, 2, HEADS + 1])
        nbias = sb("nbias", [P, TILES])
        p32 = sb("p32", [P, RING, MICRO])
        p_hi = sb("p_hi", [P, RING, MICRO], f32r)
        p_lo = sb("p_lo", [P, RING, MICRO], f32r)
        rqk = sb("rqk", [P, 2 * INNER])
        x1 = sb("x1", [P, GROUP + 1, DIM])
        v_own = sb("v_own", [P, GROUP, HEADS, HV])
        v_mix = sb("v_mix", [P, GROUP, HEADS, HV])
        sc = sb("sc", [P, HEADS * P])
        pr = sc
        prT = q16[:, :, :, :, :].rearrange("p a h k d -> p (a h k d)").bitcast(f32)\
            .rearrange("p (h n) -> p h n", n=P)
        o = sb("o", [P, INNER])
        oT = sb("oT", [P, PAIRS, P])
        h2 = sb("h2", [P, GROUP, DIM])
        h2T = sb("h2T", [P, GROUP * P])
        gT = sb("gT", [P, CH, GROUP * P])
        hT = sb("hT", [P, 2, P + 1])
        rot = sq
        qT = sb("qT", [P, PAIRS, P])
        kT = sb("kT", [P, 2, PAIRS, HALF + P])
        mx = sb("mx", [P, HEADS])
        frd = sb("frd", [P, HEADS])
        fbn = sb("fbn", [P, GROUP, 6])
        fmean = sb("fmean", [P, GROUP])
        fscr = sb("fscr", [P, 3, GROUP])
        fvar = sb("fvar", [P, GROUP])
        frs = sb("frs", [P, GROUP])


        psX = ctx.enter_context(nc.psum_tensor("psX", [P, 1024], f32))
        psY = ctx.enter_context(nc.psum_tensor("psY", [P, 1024], f32))
        psZ = ctx.enter_context(nc.psum_tensor("psZ", [P, 512], f32))
        psS = ctx.enter_context(nc.psum_tensor("psS", [P, 2, MICRO], f32))
        psV = ctx.enter_context(nc.psum_tensor("psV", [P, 512], f32))
        head_of = [psX, psY]

        first_weights = sem("first_weights")
        all_weights = sem("all_weights")
        x_arrived = sem("x_arrived")
        w1_arrived = sem("w1_arrived")
        out_written = sem("out_written")
        own_steps = sem("own_steps")
        cleared = sem("cleared")
        roots_done = sem("roots_done")
        roots_asked = sem("roots_asked")
        table_scaled = sem("table_scaled")
        a_staged = sem("a_staged")
        a_turned = sem("a_turned")
        a_stationary = sem("a_stationary")
        normed = sem("normed")
        a_projected = sem("a_projected")
        a_squared = sem("a_squared")
        a_vhigh = sem("a_vhigh")
        a_psum_free = sem("a_psum_free")
        a_parts = sem("a_parts")
        a_qkT_psum = sem("a_qkT_psum")
        a_qkT = sem("a_qkT")
        a_scores = sem("a_scores")
        a_exps = sem("a_exps")
        a_lows = sem("a_lows")
        a_products = sem("a_products")
        a_sum = sem("a_sum")
        a_pair = sem("a_pair")
        a_out_turned = sem("a_out_turned")
        a_outT = sem("a_outT")
        a_linear = sem("a_linear")
        a_done = sem("a_done")
        f_staged = sem("f_staged")
        f_turned = sem("f_turned")
        f_shifted = sem("f_shifted")
        f_projected = sem("f_projected")
        f_squared = sem("f_squared")
        f_kept = sem("f_kept")
        f_unit = sem("f_unit")
        f_sines = sem("f_sines")
        f_cosines = sem("f_cosines")
        f_rotated = sem("f_rotated")
        f_qkT_psum = sem("f_qkT_psum")
        f_qkT = sem("f_qkT")
        f_scores = sem("f_scores")
        f_less_max = sem("f_less_max")
        f_exps = sem("f_exps")
        f_weightsT_psum = sem("f_weightsT_psum")
        f_weightsT = sem("f_weightsT")
        f_products = sem("f_products")
        f_averaged = sem("f_averaged")
        f_outT_psum = sem("f_outT_psum")
        f_outT = sem("f_outT")
        f_linear = sem("f_linear")
        f_residual = sem("f_residual")
        m_shifted = sem("m_shifted")
        m_normed = sem("m_normed")
        m_turned = sem("m_turned")
        m_stationary = sem("m_stationary")
        m_up = sem("m_up")
        m_gelu = sem("m_gelu")
        m_gated = sem("m_gated")
        m_down = sem("m_down")
        m_stored = sem("m_stored")
        e_q = sem("e_q")
        e_pow = sem("e_pow")
        e_e = sem("e_e")
        e_v = sem("e_v")
        e_w = sem("e_w")
        e_out = sem("e_out")

        START = RING
        counters = [
            a_turned, a_stationary, a_exps, a_psum_free, a_lows, a_done, a_pair, a_out_turned, a_outT, a_sum,
            a_projected, a_products, a_scores, a_parts, a_squared, a_staged, a_qkT_psum, a_qkT, a_vhigh, a_linear,
            f_sines, f_cosines, f_exps, f_shifted, f_unit, f_averaged, f_outT_psum, f_outT, f_weightsT_psum,
            f_weightsT, f_projected, f_products, f_rotated, f_scores, f_squared, f_staged, f_less_max, f_qkT_psum,
            f_qkT, f_kept, f_linear, f_residual, f_turned, m_turned, m_stationary, m_down, m_gelu, m_gated,
            m_normed, m_shifted, m_up, m_stored
        ]

        block = ctx.enter_context(nc.Block())

        W_FIRST = 5
        N_W, N_W2 = 16 * W_FIRST, 16 * (16 - W_FIRST + DEPTH * (13 + 2 * CH))

        NEXT = ("stage", "load", "lanes", "project", "square", "lengths", "root", "norm", "cosine", "sine", "rotate",
                "keep")
        STEP = """stage micro load lanes micro T copyqk project square scores lengths maximum keep micro micro
                 root exp micro probs copyprobs norm micro sine values average micro turn copyo cosine micro
                 output residual rotate""".split()
        FIRST_STEP = """stage T copyqk micro load scores lanes maximum micro exp project square probs copyprobs lengths
                 micro micro keep values root average micro norm turn copyo sine micro turnA0 output cosine
                 copyA0 residual outputA0 statsA0 rotate""".split()
        LAST_STEP = """stage turnA1 copyA1 outputA1 load statsA1 T lanes copyqk micro scores maximum micro project exp
                 square probs copyprobs lengths micro root values average keep micro norm turn sine copyo micro
                 output residual micro shift mstats mroot mnorm micro micro micro cosine turnh copyh up0 up1
                 gelu0 gate0 gelu1 up2 gelu2 rotate gate1 gate2 micro down store""".split()

        OUTPUT = ("ostats", "oroot", "oexp", "odenom", "oinv", "osilu", "ogain", "oput")
        OUTPUT_AT = {2: ("ostats", 0), 3: ("oroot", 0), 4: ("oexp", 0), 6: ("odenom", 0), 7: ("oinv", 0),
                     9: ("oinv", 1), 11: ("oinv", 2), 13: ("osilu", 0), 15: ("ogain", 0), 17: ("oput", 0),
                     19: ("oput", 1), 21: ("oput", 2)}

        def group_events(last):
            m = 0
            for u in range(GROUP):
                for kind in (FIRST_STEP if u == 0 else LAST_STEP if u == GROUP - 1 else STEP):
                    if kind == "micro":
                        if not last or m < CPG - SHIFT:
                            yield kind, m + SHIFT
                        if last and m in OUTPUT_AT:
                            yield OUTPUT_AT[m]
                        m += 1
                    elif kind in NEXT:
                        if not last or u + 1 < GROUP:
                            yield kind, u + 1
                    elif kind[-1] in "012":
                        yield kind[:-1], int(kind[-1])
                    else:
                        yield kind, u
            assert m == CPG

        def run(eng, do, prologue):
            prologue()
            with eng.Fori(0, GROUPS - 1) as g:
                for kind, u in group_events(False):
                    do(kind, u, g, False)
            for kind, u in group_events(True):
                do(kind, u, GROUPS - 1, True)

        def place(g, u):
            if u == GROUP:
                g, u = g + 1, 0
            r = g % (TILES // GROUP)
            return g * GROUP + u, g // (TILES // GROUP), r * GROUP + u, (g % (TB // GROUP)) * GROUP + u

        def micro_place(g, m):
            tile = m // CPT
            return g * CPG + m, g * (CPG // CPT) + tile, ((g * (CPG // CPT) + tile) // TB) * TB, \
                m // CPU % PAIRS, m % CPU

        @block.sync
        def _(sp):
            for counter in counters:
                sp.sem_inc(counter, START)
            for c in range(4):
                t = TILES // 4
                b, o0 = divmod(c * t, TB)
                sp.dma_start(x_in[:, c * t:(c + 1) * t, :],
                             x[b, o0 * P:(o0 + t) * P, :].rearrange("(t p) d -> p t d", p=P)).then_inc(x_arrived, 16)
            loads = [
                (ident[:, :], ident_in), (ng_sb[:, :], norm_g.rearrange("(p o) -> p o", o=1)),
                (wq_sb[:, :], wq), (wkv_sb[:, :], wkv), (identh[:, :], identh_in),
                (identb[:, :], mask_in[0]),
                (wout_sb[:, :, :], wout.rearrange("(c p) n -> p c n", p=P)),
                (og_sb[:, :], out_norm_g.rearrange("(o d) -> o d", o=1).to_broadcast([P, DIM])),
                (wqkv_sb[:, :, :], wqkv.rearrange("l p n -> p l n")),
                (wo_sb[:, :, :, :], wo.rearrange("l (c p) n -> p l c n", p=P)),
                (mask[:, 0:1, :], mask_in[1:2].rearrange("t p n -> p t n")),
                (mask[:, 1:TB, :], mask_in[2:3].rearrange("t p n -> p t n").to_broadcast([P, TB - 1, P])),
                (shift[:, :, :], shift_in.rearrange("t p n -> p t n")),
                (keep[:, :], keep_in),
                (lng_sb[:, :], ln_g), (lnb_sb[:, :], ln_b),
            ]
            for l in range(DEPTH):
                loads += [(table[:, l, :, f, :], rope[f].rearrange("(t p) d -> p t d", p=P)) for f in range(4)]
                loads += [
                    (w2_sb[:, l, 0:CH - 1, :], w2[l, 0:(CH - 1) * P, :].rearrange("(c p) n -> p c n", p=P)),
                    (w2_sb[0:TAIL, l, CH - 1, :], w2[l, (CH - 1) * P:HID, :]),
                    (w2_sb[TAIL:TAIL + 1, l, CH - 1, :], b2[l:l + 1, :]),
                ]
                for k, v in ((0, q_scale), (1, k_scale)):
                    row = v[l:l + 1, :]
                    loads += [(qk_scale[:, l, k, :], row.to_broadcast([P, DH])),
                              (qk_scale[:, l, 2 + k, 0:DH // 2], row[:, DH // 2:DH].to_broadcast([P, DH // 2])),
                              (qk_scale[:, l, 2 + k, DH // 2:DH], row[:, 0:DH // 2].to_broadcast([P, DH // 2]))]
                for k in range(2):
                    for c in range(CH):
                        rows = P if c < CH - 1 else TAIL
                        at0 = k * HID + c * P
                        loads += [(b1_sb[0:rows, l, k, c:c + 1],
                                   b1[l, at0:at0 + rows].rearrange("(p o) -> p o", o=1))]
            assert 16 * len(loads) == N_W + N_W2
            for i, (dst, src) in enumerate(loads):
                sp.dma_start(dst, src).then_inc(first_weights if i < W_FIRST else all_weights, 16)
            with sp.Fori(0, DEPTH) as l:
                sp.wait_ge(m_up, START + l * (TILES // GROUP) * 2 * CH)
                sp.dma_start(w1_sb[:, :], w1[l]).then_inc(w1_arrived, 16)
            sp.wait_ge(a_scores, START + (GROUPS - 1) * CPG)
            for c in range(4):
                t = TILES // 4
                b, o0 = divmod(c * t, TB)
                sp.dma_start(x_in[:, c * t:(c + 1) * t, :],
                             x[b, o0 * P:(o0 + t) * P, :].rearrange("(t p) d -> p t d", p=P)).then_inc(x_arrived, 16)
            for c in range(4):
                t = TILES // 4
                sp.wait_ge(e_out, c + 1)
                b, o0 = divmod(c * t, TB)
                sp.dma_start(out[b, o0 * P:(o0 + t) * P, :].rearrange("(t p) d -> p t d", p=P),
                             xs[:, c * t:(c + 1) * t, :]).then_inc(out_written, 16)
            sp.wait_ge(out_written, 64)

        @block.gpsimd
        def _(pool):
            pool.memset(neg_half[:, :], -0.5)
            pool.memset(x1[:, 0, :], 0.0)
            pool.memset(v_own[:, :, :, DH:HV], 1.0)
            pool.memset(v_mix[:, :, :, DH:HV], 1.0)
            pool.memset(v_mix[:, 0, :, 0:DH], 0.0)
            pool.memset(gT[:, CH - 1, :], 1.0)
            pool.memset(hT[:, :, :], 0.0)
            pool.memset(kT[:, :, :, :], 0.0)
            pool.memset(qn[:, 0:16 * 2], 0.0)
            pool.memset(p32[:, 0, 0:TILES], 1.0)
            pool.memset(p32[:, 0, TILES:2 * TILES], 0.0).then_inc(cleared, 1)
            for k in range(2):
                pool.wait_ge(roots_asked, k + 1)
                pool.tensor_tensor(rstd[:, :], var[:, :], neg_half[:, 0:TILES], ALU.pow).then_inc(roots_done, 1)
            assert DEPTH * 4 == TILES // 2
            with pool.Fori(0, DEPTH) as l:
                for f in range(4):
                    for u in range(2):
                        pool.wait_ge(roots_asked, l * 8 + (f * 2 + u + 3))
                        pool.tensor_tensor(a_rn[:, u, :], a_ss[:, u, :], neg_half[:, 0:HEADS + 1],
                                           ALU.pow).then_inc(roots_done, 1)
                    if f == 0:
                        pool.wait_ge(all_weights, N_W2)
                    pool.tensor_tensor(table[:, l, :, f, :], table[:, l, :, f, :],
                                       qk_scale[:, l, f:f + 1, :].to_broadcast([P, TB, DH]),
                                       ALU.mult).then_inc(table_scaled, 1)
            R0 = TILES + 2

            def do(kind, u, g, last):
                if kind == "root":
                    n, _, _, _ = place(g, u)
                    pool.wait_ge(roots_asked, R0 + n + g + 1)
                    pool.tensor_tensor(rn[:, :], ss[:, :], neg_half[:, :], ALU.pow).then_inc(roots_done, 1)
                elif kind == "sine":
                    n, l, _, t = place(g, u)
                    pool.wait_ge(f_unit, START + n + 1)
                    src = qn[:, :].rearrange("p (k h d) -> p k h d", k=2, d=DH)
                    dst = rot[:, :].rearrange("p (k h d) -> p k h d", k=2, d=DH)
                    hd = DH // 2
                    for k in range(2):
                        for a, c in ((0, hd), (hd, 0)):
                            final = pool.tensor_tensor(
                                dst[:, k, :, a:a + hd], src[:, k, :, c:c + hd],
                                table[:, l, t, 2 + k:3 + k, a:a + hd].to_broadcast([P, HEADS, hd]), ALU.mult)
                    final.then_inc(f_sines, 1)
                elif kind == "mroot":
                    ready = g * (GROUP + 1) + GROUP + (1 if last else 2)
                    pool.wait_ge(roots_asked, R0 + ready)
                    pool.tensor_tensor(frs[:, :], fvar[:, :], neg_half[:, 0:GROUP], ALU.pow).then_inc(roots_done, 1)
                elif kind == "oroot":
                    out_roots(0, EARLY)

            def out_roots(lo, hi):
                pool.wait_ge(e_q, 1 if lo == 0 else 2)
                pool.tensor_tensor(rstd[:, lo:hi], var[:, lo:hi], neg_half[:, 0:hi - lo], ALU.pow).then_inc(e_pow, 1)

            def prologue():
                do("root", 0, 0, False)
                do("sine", 0, 0, False)

            run(pool, do, prologue)
            out_roots(EARLY, TILES)

        @block.scalar
        def _(act):
            act.wait_ge(first_weights, N_W)

            def stage(t, u):
                act.wait_ge(a_turned, START + t - 1)
                act.activation(xst[:, u, :], xs[:, t, :], ACT.Identity, scale=rstd[:, bass.ds(t, 1)],
                               bias=nbias[:, bass.ds(t, 1)]).then_inc(a_staged, 1)

            def turned(t, u):
                act.wait_ge(a_turned, START + t + 1)
                act.activation(aT[:, u, :], psZ[:, 0:P], ACT.Copy, scale=ng_sb[:, 0:1]).then_inc(a_stationary, 1)

            def squares(t, u):
                act.wait_ge(a_projected, START + t + 1)
                act.wait_ge(roots_asked, t + 2)
                act.activation(sq[:, 0:INNER + DH], head_of[u][:, 0:INNER + DH], ACT.Square).then_inc(a_squared, 1)
                act.activation(v_r[:, t, 0:DH], head_of[u][:, INNER + DH:INNER + 2 * DH], ACT.Copy).then_inc(a_vhigh, 1)

            def back(t, u):
                act.wait_ge(a_qkT_psum, START + t + 1)
                act.activation(qT16[:, t, :, :], psS[:, 0, :].bitcast(f16), ACT.Copy)
                act.activation(kT16[:, t, :, :], psS[:, 1, 0:P].bitcast(f16), ACT.Copy).then_inc(a_qkT, 1)

            act.wait_ge(normed, 1)
            stage(0, 0)
            turned(0, 0)
            stage(1, 1)
            squares(0, 0)
            turned(1, 1)
            stage(2, 0)
            squares(1, 1)
            turned(2, 0)
            with act.Fori(0, TILES // 2 - 2) as i:
                for u in range(2):
                    stage(i * 2 + u + 3, 1 - u)
                    squares(i * 2 + u + 2, u)
                    turned(i * 2 + u + 3, 1 - u)
                    back(i * 2 + u, u)
            stage(TILES - 1, 1)
            squares(TILES - 2, 0)
            turned(TILES - 1, 1)
            back(TILES - 4, 0)
            squares(TILES - 1, 1)
            back(TILES - 3, 1)

            def do(kind, u, g, last):
                if kind == "micro":
                    if last and u + AHEAD >= CPG:
                        return
                    m, _, _, _, _ = micro_place(g, u + AHEAD)
                    exponentials(m, u + AHEAD)
                    return
                n, l, tile, _ = place(g, u)
                if kind == "stage":
                    load(n, tile, g, u)
                elif kind == "square":
                    act.wait_ge(f_projected, START + n + 1)
                    act.wait_ge(f_rotated, START + n)
                    act.activation(sq[:, :], psX[:, :], ACT.Square).then_inc(f_squared, 1)
                elif kind == "keep":
                    src = psZ[:, 0:INNER].rearrange("p (h d) -> p h d", d=DH)
                    act.wait_ge(f_products, START + n - 2)
                    act.activation(v_own[:, u % GROUP, :, 0:DH], src, ACT.Copy)
                    act.activation(v_mix[0:HALF, u % GROUP, :, 0:DH], src[0:HALF], ACT.Copy)
                    act.activation(v_mix[HALF:P, (u + 1) % GROUP, :, 0:DH], src[HALF:P], ACT.Copy).then_inc(f_kept, 1)
                elif kind == "copyqk":
                    act.wait_ge(f_qkT_psum, START + n + 1)
                    act.wait_ge(f_scores, START + n)
                    act.activation(qT[:, :, :], psY[:, 0:512], ACT.Copy)
                    k_ps = psY[:, 512:1024].rearrange("p (k n) -> p k n", n=P)
                    act.activation(kT[:, u % 2, :, 0:P], k_ps, ACT.Copy)
                    act.activation(kT[:, (u + 1) % 2, :, P:P + HALF], k_ps[:, :, HALF:P], ACT.Copy).then_inc(f_qkT, 1)
                elif kind == "exp":
                    act.wait_ge(f_less_max, START + n + 1)
                    act.wait_ge(f_weightsT_psum, START + n)
                    act.activation(pr[:, :], sc[:, :], ACT.Exp).then_inc(f_exps, 1)
                elif kind == "copyprobs":
                    act.wait_ge(f_weightsT_psum, START + n + 1)
                    act.wait_ge(f_products, START + n)
                    act.activation(prT[:, :, :], psY[:, :], ACT.Copy).then_inc(f_weightsT, 1)
                elif kind == "copyo":
                    act.wait_ge(f_outT_psum, START + n + 1)
                    act.wait_ge(f_linear, START + n)
                    act.activation(oT[:, :, :], psZ[:, 0:512], ACT.Copy).then_inc(f_outT, 1)
                elif kind == "copyh":
                    act.wait_ge(m_turned, START + g + 1)
                    act.activation(h2T[:, :], psZ[:, 0:512], ACT.Identity, scale=lng_sb[:, bass.ds(l, 1)],
                                   bias=lnb_sb[:, bass.ds(l, 1)]).then_inc(m_stationary, 1)
                elif kind == "gelu":
                    c = u
                    _, l, _, _ = place(g, 0)
                    rows = P if c < CH - 1 else TAIL
                    act.wait_ge(m_up, START + g * 2 * CH + 2 * c + 2)
                    act.wait_ge(m_down, START + g)
                    act.activation(gT[0:rows, c, :], (psX, psY)[c % 2][0:rows, 512:1024], ACT.Gelu,
                                   bias=b1_sb[0:rows, l, 1, c:c + 1]).then_inc(m_gelu, 1)
                elif kind == "oexp":
                    silu_exp(0, EARLY)
                elif kind == "copyA":
                    t = g * (CPG // CPT) + u
                    act.wait_ge(a_out_turned, START + t + 1)
                    act.activation(oaT[:, :, :], psY[:, 0:512], ACT.Copy).then_inc(a_outT, 1)

            def silu_exp(lo, hi):
                act.wait_ge(m_stored, START + GROUPS - (1 if lo == 0 else 0))
                act.wait_ge(a_scores, START + (GROUPS - 1) * CPG)
                act.activation(e_silu[:, lo * DIM:hi * DIM], xs[:, lo:hi, :].rearrange("p t d -> p (t d)"),
                               ACT.Exp, scale=-1.0).then_inc(e_e, 1)

            def exponentials(m, j):
                act.wait_ge(a_scores, START + m + 1)
                act.wait_ge(a_products, START + m - RING + 1)
                act.activation(p32[:, j % RING, :], psS[:, j % 2, :], ACT.Exp, scale=ATT_SCALE)
                act.activation(p_hi[:, j % RING, :], psS[:, j % 2, :], ACT.Exp, scale=ATT_SCALE).then_inc(a_exps, 1)

            def load(n, tile, g, u):
                act.wait_ge(m_stored, START + g)
                act.wait_ge(f_turned, START + n - 1)
                act.activation(xst[:, u % 2, :], xs[:, tile, :], ACT.Copy).then_inc(f_staged, 1)

            def prologue():
                load(0, 0, 0, 0)
                back(TILES - 2, 0)
                act.wait_ge(all_weights, N_W2)
                do("square", 0, 0, False)
                back(TILES - 1, 1)
                do("keep", 0, 0, False)
                for m in range(AHEAD):
                    exponentials(m, m)
                for m in range(SHIFT):
                    do("micro", m, 0, False)

            run(act, do, prologue)
            silu_exp(EARLY, TILES)

        @block.vector
        def _(dve):
            DVE = nc.vector

            class Chain:
                base = 0
                n = 0

            ch = Chain()

            def link(ins):
                ch.n += 1
                ins.then_inc(own_steps, 1)
                dve.wait_ge(own_steps, ch.base + ch.n)

            def statistics(stats, mean, variance, scratch):
                m0, m1, q0, q1 = (stats[:, :, c] for c in (1, 4, 2, 5))
                d, d2, m2 = (scratch[:, c, :] for c in range(3))
                DVE.tensor_tensor(mean, m0, m1, ALU.add)
                DVE.tensor_tensor(d, m0, m1, ALU.subtract)
                link(DVE.tensor_tensor(m2, q0, q1, ALU.add))
                DVE.tensor_scalar(mean, mean, 0.5, None, ALU.mult)
                DVE.tensor_scalar(m2, m2, 1.0 / DIM, EPS, ALU.mult, ALU.add)
                link(DVE.scalar_tensor_tensor(d2, d, 0.25, d, ALU.mult, ALU.mult))
                return DVE.tensor_tensor(variance, m2, d2, ALU.add)

            HALF_TILES = TILES // 2

            def half_stats(src, c):
                for j in range(HALF_TILES):
                    last = DVE.bn_stats(bn[:, c * HALF_TILES + j, :], src[:, c * HALF_TILES + j, :])
                last.then_inc(own_steps, 1)

            def root(k):
                statistics(bn, mean[:, :], var[:, :], scr).then_inc(roots_asked, 1)
                dve.wait_ge(roots_done, k + 1)

            dve.wait_ge(cleared, 1)
            DVE.tensor_copy(v_r[:, :, 2 * DH:VW - 1], p32[:, 0, 0:TILES].unsqueeze(2))
            DVE.tensor_copy(v_r[:, :, VW - 1:VW], p32[:, 0, TILES:2 * TILES].unsqueeze(2)).then_inc(a_parts, 1)
            dve.wait_ge(x_arrived, 64)
            with dve.Fori(0, 2) as c:
                half_stats(x_in, c)
            dve.wait_ge(own_steps, 2)
            ch.base = 2
            root(0)
            base0 = ch.base + ch.n
            with dve.Fori(0, 2) as c:
                for j in range(HALF_TILES):
                    t = c * HALF_TILES + j
                    last = DVE.tensor_scalar(xs[:, t, :], x_in[:, t, :], mean[:, bass.ds(t, 1)], rstd[:, bass.ds(t, 1)],
                                             ALU.subtract, ALU.mult)
                last.then_inc(own_steps, 1)
                dve.wait_ge(own_steps, base0 + c * 2 + 1)
                half_stats(xs, c)
            ch.base = ch.base + 4
            dve.wait_ge(own_steps, ch.base + ch.n)
            root(1)
            DVE.scalar_tensor_tensor(nbias[:, :], mean[:, :], -1.0, rstd[:, :], ALU.mult, ALU.mult).then_inc(normed, 1)
            ch.base, ch.n = ch.base + ch.n, 0
            A_STEPS = 3

            def lengths(t, u, step):
                dve.wait_ge(a_squared, START + t + 1)
                DVE.tensor_reduce(a_ss[:, u, :], sq[:, 0:INNER + DH].rearrange("p (h d) -> p h d", d=DH),
                                  AX.X, ALU.add).then_inc(own_steps, 1)
                dve.wait_ge(own_steps, step + 1)
                DVE.tensor_scalar(a_ss[:, u, :], a_ss[:, u, :], 1 / QS ** 2, TINY / QS ** 2, ALU.mult,
                                  ALU.max).then_inc(roots_asked, 1)

            def take(t, u):
                dve.wait_ge(a_vhigh, START + t + 1)
                dve.wait_ge(roots_done, t + 3)
                dve.wait_ge(a_parts, START + t + 1)
                DVE.tensor_tensor(qn[:, 0:INNER + DH].rearrange("p (h d) -> p h d", d=DH),
                                  head_of[u][:, 0:INNER + DH].rearrange("p (h d) -> p h d", d=DH),
                                  a_rn[:, u, :].unsqueeze(2).to_broadcast([P, HEADS + 1, DH]),
                                  ALU.mult).then_inc(own_steps, 1)
                DVE.tensor_tensor(v_r[:, t, DH:2 * DH], head_of[u][:, INNER + DH:INNER + 2 * DH],
                                  v_r[:, t, 0:DH].bitcast(f32), ALU.subtract).then_inc(a_psum_free, 1)

            def parts(t, u, taken, step):
                dve.wait_ge(own_steps, taken)
                dve.wait_ge(a_qkT_psum, START + t - 1)
                qf = qn[:, 0:INNER].rearrange("p (h d) -> p h d", d=DH)
                kf = qn[:, INNER:INNER + DH].unsqueeze(1).to_broadcast([P, 2, DH])
                krows = k16[:, u, :, :, :].rearrange("p a b d -> p (a b) d")
                DVE.tensor_copy(q16[:, u, :, 0, :], qf)
                DVE.tensor_copy(krows[:, 0:4:3, :], kf).then_inc(own_steps, 1)
                dve.wait_ge(own_steps, step + 1)
                DVE.tensor_tensor(q16[:, u, :, 1, :], qf, q16[:, u, :, 0, :], ALU.subtract)
                DVE.tensor_tensor(krows[:, 1:3, :], kf, krows[:, 0:4:3, :], ALU.subtract).then_inc(a_parts, 1)

            lengths(0, 0, ch.base)
            base0 = ch.base + 1
            with dve.Fori(0, TILES // 2 - 1) as i:
                for u in range(2):
                    step = base0 + (i * 2 + u) * A_STEPS
                    take(i * 2 + u, u)
                    lengths(i * 2 + u + 1, 1 - u, step + 1)
                    parts(i * 2 + u, u, step + 1, step + 2)
            step = base0 + (TILES - 2) * A_STEPS
            take(TILES - 2, 0)
            lengths(TILES - 1, 1, step + 1)
            ch.base, ch.n = step + 5, 0

            R0 = TILES + 2
            dve.wait_ge(table_scaled, DEPTH * 4)
            dve.wait_ge(all_weights, N_W2)

            def heads(t, k=HEADS):
                return t.rearrange("p (h d) -> p h d", h=k)

            def split(m, j):
                dve.wait_ge(a_exps, START + m + 1)
                DVE.tensor_tensor(p_lo[:, j % RING, :], p32[:, j % RING, :], p_hi[:, j % RING, :].bitcast(f32),
                                  ALU.subtract).then_inc(a_lows, 1)

            def average(g, j):
                _, t, _, hp, _ = micro_place(g, j)
                unit = g * (CPG // CPU) + j // CPU
                dve.wait_ge(a_products, START + (unit + 1) * CPU)
                if hp == 0:
                    dve.wait_ge(a_out_turned, START + t)
                pv = heads(psV[:, 0:2 * VW], 2)
                DVE.reciprocal(rden[:, 0:2], pv[:, :, 2 * DH])
                DVE.tensor_reduce(oa[:, 2 * hp:2 * hp + 2, :],
                                  pv[:, :, 0:2 * DH].rearrange("p h (a d) -> p h d a", a=2), AX.X,
                                  ALU.add).then_inc(a_sum, 1)
                dve.wait_ge(a_sum, START + unit + 1)
                DVE.tensor_tensor(oa[:, 2 * hp:2 * hp + 2, :], oa[:, 2 * hp:2 * hp + 2, :],
                                  rden[:, 0:2].unsqueeze(2).to_broadcast([P, 2, DH]), ALU.mult).then_inc(a_pair, 1)

            def do(kind, u, g, last):
                if kind == "micro":
                    if not (last and u + AHEAD >= CPG):
                        m, _, _, _, _ = micro_place(g, u + AHEAD)
                        split(m, u + AHEAD)
                    if u % CPU == CPU - 1:
                        average(g, u)
                    return
                n, l, tile, t = place(g, u)
                if kind == "lanes":
                    dve.wait_ge(f_turned, START + n + 1)
                    dve.wait_ge(f_projected, START + n)
                    DVE.tensor_copy(hT[0:HALF, u % 2, 0:P], psZ[0:HALF, 0:P])
                    DVE.tensor_copy(hT[HALF:P, u % 2, 1:P + 1], psZ[HALF:P, 0:P])
                    nxt = hT[HALF:P, (u + 1) % 2, 0:1]
                    if u % GROUP < GROUP - 1:
                        DVE.tensor_copy(nxt, psZ[HALF:P, P - 1:P]).then_inc(f_shifted, 1)
                    else:
                        DVE.tensor_scalar(nxt, psZ[HALF:P, P - 1:P], keep[HALF:P, bass.ds(g % (TB // GROUP), 1)],
                                          None, ALU.mult).then_inc(f_shifted, 1)
                elif kind == "lengths":
                    dve.wait_ge(f_squared, START + n + 1)
                    link(DVE.tensor_reduce(ss[:, :], heads(sq[:, :], 2 * HEADS), AX.X, ALU.add))
                    DVE.tensor_scalar(ss[:, :], ss[:, :], TINY, None, ALU.max).then_inc(roots_asked, 1)
                elif kind == "norm":
                    dve.wait_ge(roots_done, R0 + n + g + 1)
                    dve.wait_ge(f_sines, START + n)
                    DVE.tensor_tensor(heads(qn[:, :], 2 * HEADS), heads(psX[:, :], 2 * HEADS),
                                      rn[:, :].unsqueeze(2).to_broadcast([P, 2 * HEADS, DH]),
                                      ALU.mult).then_inc(f_unit, 1)
                elif kind == "cosine":
                    dve.wait_ge(f_unit, START + n + 1)
                    dve.wait_ge(f_qkT_psum, START + n)
                    for k in range(2):
                        part = slice(k * INNER, (k + 1) * INNER)
                        final = DVE.tensor_tensor(heads(rqk[:, part]), heads(qn[:, part]),
                                                  table[:, l, t, k:k + 1, :].to_broadcast([P, HEADS, DH]), ALU.mult)
                    final.then_inc(f_cosines, 1)
                elif kind == "rotate":
                    dve.wait_ge(f_cosines, START + n + 1)
                    dve.wait_ge(f_sines, START + n + 1)
                    DVE.tensor_tensor(rqk[:, :], rqk[:, :], rot[:, :], ALU.add).then_inc(f_rotated, 1)
                elif kind == "maximum":
                    dve.wait_ge(f_scores, START + n + 1)
                    s3 = heads(psY[:, :])
                    link(DVE.tensor_reduce(mx[:, :], s3, AX.X, ALU.max))
                    dve.wait_ge(f_exps, START + n)
                    DVE.tensor_tensor(heads(sc[:, :]), s3, mx[:, :].unsqueeze(2).to_broadcast([P, HEADS, P]),
                                      ALU.subtract).then_inc(f_less_max, 1)
                elif kind == "average":
                    dve.wait_ge(f_products, START + n + 1)
                    pv = psY[:, :].rearrange("p (k n) -> p k n", k=2)[:, :, 0:PAIRS * HV]\
                        .rearrange("p k (h v) -> p k h v", v=HV)
                    link(DVE.reciprocal(frd[:, :].rearrange("p (k h) -> p k h", k=2), pv[:, :, :, DH]))
                    dve.wait_ge(f_outT_psum, START + n)
                    for k in range(2):
                        final = DVE.tensor_tensor(
                            heads(o[:, k * INNER // 2:(k + 1) * INNER // 2], PAIRS), pv[:, k, :, 0:DH],
                            frd[:, k * PAIRS:(k + 1) * PAIRS].unsqueeze(2).to_broadcast([P, PAIRS, DH]), ALU.mult)
                    final.then_inc(f_averaged, 1)
                elif kind == "residual":
                    dve.wait_ge(f_linear, START + n + 1)
                    DVE.tensor_tensor(x1[:, u + 1, :], psZ[:, 0:DIM], xs[:, tile, :], ALU.add).then_inc(f_residual, 1)
                elif kind == "mstats":
                    dve.wait_ge(m_shifted, START + g + 1)
                    DVE.tensor_scalar(h2[:, :, 0:HALF], x1[:, 1:GROUP + 1, 0:HALF], 1.0, None, ALU.mult)
                    link(DVE.tensor_copy(h2[:, :, HALF:P], heads(psZ[:, 0:GROUP * HALF], GROUP)))
                    for i in range(GROUP):
                        final = DVE.bn_stats(fbn[:, i, :], h2[:, i, :])
                    link(final)
                    statistics(fbn, fmean[:, :], fvar[:, :], fscr).then_inc(roots_asked, 1)
                elif kind == "mnorm":
                    dve.wait_ge(roots_done, R0 + g * (GROUP + 1) + GROUP + (1 if last else 2))
                    for i in range(GROUP):
                        final = DVE.tensor_scalar(h2[:, i, :], h2[:, i, :], fmean[:, i:i + 1], frs[:, i:i + 1],
                                                  ALU.subtract, ALU.mult)
                    final.then_inc(m_normed, 1)
                elif kind == "gate":
                    c = u
                    _, l, _, _ = place(g, 0)
                    rows = P if c < CH - 1 else TAIL
                    dve.wait_ge(m_gelu, START + g * CH + c + 1)
                    DVE.scalar_tensor_tensor(gT[0:rows, c, :], (psX, psY)[c % 2][0:rows, 0:512],
                                             b1_sb[0:rows, l, 0, c:c + 1], gT[0:rows, c, :], ALU.add,
                                             ALU.mult).then_inc(m_gated, 1)
                elif kind == "store":
                    tile = place(g, 0)[2]
                    dve.wait_ge(m_down, START + g + 1)
                    DVE.tensor_tensor(xs[:, bass.ds(tile, GROUP), :], x1[:, 1:GROUP + 1, :],
                                      heads(psZ[:, 0:GROUP * P], GROUP), ALU.add).then_inc(m_stored, 1)
                    link(DVE.tensor_scalar(x1[:, 0, HALF:P], x1[:, GROUP, HALF:P],
                                           keep[:, bass.ds(g % (TB // GROUP), 1)], None, ALU.mult))
                elif kind in OUTPUT:
                    output(kind + (str(u) if kind in ("oput", "oinv") else ""), 0, EARLY)
                elif kind == "statsA":
                    t = g * (CPG // CPT) + u
                    dve.wait_ge(a_linear, START + t + 1)
                    DVE.tensor_scalar(xnn[:, t, :], psY[:, 512:512 + DIM], 1.0, None, ALU.mult)
                    DVE.bn_stats(bn[:, t, :], psY[:, 512:512 + DIM]).then_inc(a_done, 1)

            def prologue():
                parts(TILES - 2, 0, step + 1, step + 2)
                do("lanes", 0, 0, False)
                take(TILES - 1, 1)
                parts(TILES - 1, 1, step + 4, step + 4)
                do("lengths", 0, 0, False)
                for m in range(AHEAD):
                    split(m, m)
                do("norm", 0, 0, False)
                do("cosine", 0, 0, False)
                for m in range(SHIFT):
                    if m == 2:
                        do("rotate", 0, 0, False)
                    do("micro", m, 0, False)

            def output(kind, lo, hi):
                e = e_silu[:, lo * DIM:hi * DIM]
                e3 = e.rearrange("p (t d) -> p t d", d=DIM)
                pieces = (hi - lo) // GROUP
                before = 0 if lo == 0 else 3 + EARLY // GROUP
                if kind == "ostats":
                    dve.wait_ge(a_done, START + hi)
                    statistics(bn[:, lo:hi, :], mean[:, lo:hi], var[:, lo:hi], scr[:, :, lo:hi]).then_inc(e_q, 1)
                elif kind == "odenom":
                    dve.wait_ge(e_e, 1 if lo == 0 else 2)
                    DVE.tensor_scalar(e, e, 1.0, None, ALU.add).then_inc(e_v, 1)
                elif kind[:-1] == "oinv":
                    dve.wait_ge(e_v, before + 1)
                    c = int(kind[-1])
                    piece = e_silu[:, c * GROUP * DIM:(c + 1) * GROUP * DIM]
                    DVE.reciprocal(piece, piece).then_inc(e_v, 1)
                elif kind == "osilu":
                    dve.wait_ge(e_v, before + 1 + pieces)
                    DVE.tensor_tensor(e3, e3, xs[:, lo:hi, :], ALU.mult).then_inc(e_v, 1)
                elif kind == "ogain":
                    dve.wait_ge(e_v, before + 2 + pieces)
                    DVE.tensor_tensor(e3, e3, og_sb[:, :].unsqueeze(1).to_broadcast([P, hi - lo, DIM]),
                                      ALU.mult).then_inc(e_v, 1)
                elif kind[:-1] == "oput":
                    c = int(kind[-1])
                    dve.wait_ge(e_v, before + 3 + pieces)
                    dve.wait_ge(e_pow, 1 if lo == 0 else 2)
                    dve.wait_ge(x_arrived, 128)
                    tiles = range(c * GROUP, c * GROUP + GROUP)
                    for t in tiles:
                        final = DVE.scalar_tensor_tensor(xnn[:, t, :], xnn[:, t, :], mean[:, t:t + 1],
                                                         e_silu[:, t * DIM:(t + 1) * DIM], ALU.subtract, ALU.mult)
                    final.then_inc(e_w, 1)
                    dve.wait_ge(e_w, c + 1)
                    for t in tiles:
                        final = DVE.scalar_tensor_tensor(xs[:, t, :], xnn[:, t, :], rstd[:, t:t + 1], x_in[:, t, :],
                                                         ALU.mult, ALU.add)
                    final.then_inc(e_out, 1)

            GROUP_STEPS = 3 * GROUP + 5
            prologue()
            base0 = ch.base + ch.n
            with dve.Fori(0, GROUPS - 1) as g:
                ch.base, ch.n = base0 + g * GROUP_STEPS, 0
                for kind, u in group_events(False):
                    do(kind, u, g, False)
                assert ch.n == GROUP_STEPS, ch.n
            ch.base, ch.n = base0 + (GROUPS - 1) * GROUP_STEPS, 0
            for kind, u in group_events(True):
                do(kind, u, GROUPS - 1, True)
            for kind in ("ostats", "odenom", "oinv3", "osilu", "ogain", "oput3"):
                output(kind, EARLY, TILES)

        @block.tensor
        def _(pe):
            PE = nc.tensor
            one = dict(start=True, stop=True)
            pe.wait_ge(first_weights, N_W)
            pe.wait_ge(normed, 1)


            def turn(t, u):
                pe.wait_ge(a_staged, START + t + 1)
                pe.wait_ge(a_stationary, START + t)
                PE.transpose(psZ[:, 0:P], xst[:, u, :], ident[:, :]).then_inc(a_turned, 1)

            def project(t, u):
                pe.wait_ge(a_stationary, START + t + 1)
                pe.wait_ge(a_psum_free, START + t - 1)
                PE.matmul(head_of[u][:, 0:INNER], aT[:, u, :], wq_sb[:, :], **one)
                PE.matmul(head_of[u][:, INNER:INNER + 2 * DH], aT[:, u, :], wkv_sb[:, :],
                          **one).then_inc(a_projected, 1)

            def back(t, u):
                pe.wait_ge(a_parts, START + t + 2)
                pe.wait_ge(a_qkT, START + t)
                for h in range(HEADS):
                    PE.transpose(psS[:, 0, h * HALF:(h + 1) * HALF].bitcast(f16),
                                 q16[:, u, h, :, :].rearrange("p a d -> p (a d)"), identh[:, :])
                for k in range(2):
                    last = PE.transpose(psS[:, 1, k * HALF:(k + 1) * HALF].bitcast(f16),
                                        k16[:, u, k, :, :].rearrange("p a d -> p (a d)"), identh[:, :])
                last.then_inc(a_qkT_psum, 1)

            turn(0, 0)
            project(0, 0)
            turn(1, 1)
            project(1, 1)
            turn(2, 0)
            with pe.Fori(0, TILES // 2 - 2) as i:
                for u in range(2):
                    project(i * 2 + u + 2, u)
                    turn(i * 2 + u + 3, 1 - u)
                    back(i * 2 + u, u)
            project(TILES - 2, 0)
            turn(TILES - 1, 1)
            back(TILES - 4, 0)
            project(TILES - 1, 1)
            back(TILES - 3, 1)

            def queries(g, j):
                m, tile, kb, hp, c = micro_place(g, j)
                pe.wait_ge(a_exps, START + m - 1)
                for k in range(2):
                    for part in range(2):
                        final = PE.matmul(psS[:, j % 2, k * 256:(k + 1) * 256], kT16[:, kb + 2 * c + k, part, :],
                                          qT16[:, tile, 2 * hp:2 * hp + 2, :], start=(part == 0), stop=(part == 1))
                final.then_inc(a_scores, 1)

            def values(g, j):
                m, _, kb, _, c = micro_place(g, j)
                if c == 0:
                    pe.wait_ge(a_pair, START + g * (CPG // CPU) + j // CPU)
                pe.wait_ge(a_lows, START + m + 1)
                for k in range(2):
                    for pi, part in enumerate((p_hi, p_lo)):
                        for h in range(2):
                            final = PE.matmul(psV[:, h * VW:(h + 1) * VW],
                                              part[:, j % RING, k * 256 + h * P:k * 256 + (h + 1) * P],
                                              v_r[:, kb + 2 * c + k, :],
                                              start=(c == 0 and k == 0 and pi == 0 and h == 0),
                                              stop=(c == CPU - 1 and k == 1 and pi == 1), skip_group_check=True)
                final.then_inc(a_products, 1)

            def do(kind, u, g, last):
                if kind == "micro":
                    if not (last and u + AHEAD >= CPG):
                        queries(g, u + AHEAD)
                    values(g, u)
                    return
                n, l, _, t = place(g, u)
                if kind == "load":
                    pe.wait_ge(f_staged, START + n + 1)
                    pe.wait_ge(f_residual, START + n - 1)
                    pe.wait_ge(m_stored, START + g)
                    PE.transpose(psZ[:, 0:P], xst[:, u % 2, :], ident[:, :]).then_inc(f_turned, 1)
                elif kind == "project":
                    pe.wait_ge(f_shifted, START + n + 1)
                    pe.wait_ge(f_unit, START + n)
                    for k, dst in enumerate((psX[:, 0:512], psX[:, 512:1024], psZ[:, :])):
                        final = PE.matmul(dst, hT[:, u % 2, 0:P], wqkv_sb[:, l, k * INNER:(k + 1) * INNER], **one)
                    final.then_inc(f_projected, 1)
                elif kind == "T":
                    pe.wait_ge(f_rotated, START + n + 1)
                    pe.wait_ge(f_averaged, START + n)
                    pe.wait_ge(a_done, START + g * (CPG // CPT) + (0 if u == 0 else 2 if u == GROUP - 1 else 1))
                    if u == 0:
                        pe.wait_ge(m_gated, START + g * CH)
                    for k in range(2 * PAIRS):
                        final = PE.transpose(psY[:, k * P:(k + 1) * P], rqk[:, k * P:(k + 1) * P], ident[:, :])
                    final.then_inc(f_qkT_psum, 1)
                elif kind == "scores":
                    pe.wait_ge(f_qkT, START + n + 1)
                    for r in range(2):
                        PE.matmul(heads(psY[:, r * 512:(r + 1) * 512], PAIRS), identb[:, :],
                                  mask[:, bass.ds(t, 1), :].to_broadcast([P, PAIRS, P]),
                                  start=True, stop=False, skip_group_check=True)
                    rows = [slice(0, HALF), slice(HALF, P)]
                    for k in range(PAIRS):
                        for r in range(2):
                            col = r * 512 + k * P
                            q, keys = qT[rows[r], k, :], kT[rows[r], u % 2, k, :]
                            acc = dict(start=False, stop=(k == PAIRS - 1), skip_group_check=True)
                            mixed = keys.rearrange("p (s n) -> p s n", n=HALF)[:, 0:3:2, :]
                            PE.matmul(psY[0:HALF, col:col + P], q[:, 0:HALF], mixed, **acc)
                            final = PE.matmul(psY[HALF:P, col:col + P], q[:, HALF:P], keys[:, 0:P], **acc)
                    final.then_inc(f_scores, 1)
                elif kind == "probs":
                    pe.wait_ge(f_exps, START + n + 1)
                    for k in range(HEADS):
                        final = PE.transpose(psY[:, k * P:(k + 1) * P], pr[:, k * P:(k + 1) * P], ident[:, :])
                    final.then_inc(f_weightsT_psum, 1)
                elif kind == "values":
                    pe.wait_ge(f_weightsT, START + n + 1)
                    for h in range(HEADS):
                        at = (h % 2) * PAIRS + h // 2
                        col = (h // PAIRS) * 512 + (h % PAIRS) * HV
                        PE.matmul(psY[0:HALF, col:col + HV], prT[:, at, 0:HALF], v_mix[:, u, h, :], **one)
                        final = PE.matmul(psY[HALF:P, col:col + HV], prT[:, at, HALF:P], v_own[:, u, h, :], **one)
                    final.then_inc(f_products, 1)
                elif kind == "turn":
                    pe.wait_ge(f_averaged, START + n + 1)
                    pe.wait_ge(f_kept, START + n + (1 if last and u == GROUP - 1 else 2))
                    for k in range(PAIRS):
                        final = PE.transpose(psZ[:, k * P:(k + 1) * P], o[:, k * P:(k + 1) * P], ident[:, :])
                    final.then_inc(f_outT_psum, 1)
                elif kind == "output":
                    pe.wait_ge(f_outT, START + n + 1)
                    for k in range(PAIRS):
                        final = PE.matmul(psZ[:, 0:DIM], oT[:, k, :], wo_sb[:, l, k, :],
                                          start=(k == 0), stop=(k == PAIRS - 1))
                    final.then_inc(f_linear, 1)
                elif kind == "shift":
                    pe.wait_ge(f_residual, START + g * GROUP + GROUP)
                    for i in range(GROUP):
                        dst = psZ[:, i * HALF:(i + 1) * HALF]
                        PE.matmul(dst, shift[:, 0, :], x1[:, i + 1, HALF:P], start=True, stop=False)
                        final = PE.matmul(dst, shift[:, 1, :], x1[:, i, HALF:P], start=False, stop=True)
                    final.then_inc(m_shifted, 1)
                elif kind == "turnh":
                    pe.wait_ge(m_normed, START + g + 1)
                    for i in range(GROUP):
                        final = PE.transpose(psZ[:, i * P:(i + 1) * P], h2[:, i, :], ident[:, :])
                    final.then_inc(m_turned, 1)
                elif kind == "up":
                    c = u
                    _, l, _, _ = place(g, 0)
                    pe.wait_ge(m_stationary, START + g + 1)
                    pe.wait_ge(w1_arrived, l * 16 + 16)
                    pe.wait_ge(f_unit, START + g * GROUP + GROUP + (0 if last else 1))
                    pe.wait_ge(f_averaged, START + g * GROUP + GROUP)
                    rows = P if c < CH - 1 else TAIL
                    if c >= 2:
                        pe.wait_ge(m_gated, START + g * CH + c - 1)
                    for k in range(2):
                        PE.matmul((psX, psY)[c % 2][0:rows, k * 512:(k + 1) * 512],
                                  w1_sb[:, k * HID + c * P:k * HID + c * P + rows], h2T[:, :],
                                  **one).then_inc(m_up, 1)
                elif kind == "down":
                    pe.wait_ge(m_gated, START + g * CH + CH)
                    for i in range(GROUP):
                        for c in range(CH):
                            rows = P if c < CH - 1 else TAIL + 1
                            final = PE.matmul(psZ[:, i * P:(i + 1) * P], gT[0:rows, c, i * P:(i + 1) * P],
                                              w2_sb[0:rows, l, c, :], start=(c == 0), stop=(c == CH - 1))
                    final.then_inc(m_down, 1)
                elif kind == "turnA":
                    t = g * (CPG // CPT) + u
                    pe.wait_ge(a_pair, START + (t + 1) * PAIRS)
                    pe.wait_ge(f_averaged, START + g * GROUP + (1 if u == 0 else GROUP - 1))
                    oflat = oa[:, :, :].rearrange("p h d -> p (h d)")
                    for k in range(PAIRS):
                        final = PE.transpose(psY[:, k * P:(k + 1) * P], oflat[:, k * P:(k + 1) * P], ident[:, :])
                    final.then_inc(a_out_turned, 1)
                elif kind == "outputA":
                    t = g * (CPG // CPT) + u
                    pe.wait_ge(a_outT, START + t + 1)
                    for k in range(PAIRS):
                        final = PE.matmul(psY[:, 512:512 + DIM], oaT[:, k, :], wout_sb[:, k, :],
                                          start=(k == 0), stop=(k == PAIRS - 1))
                    final.then_inc(a_linear, 1)

            def heads(t, k):
                return t.rearrange("p (h d) -> p h d", h=k)

            def prologue():
                do("load", 0, 0, False)
                back(TILES - 2, 0)
                do("project", 0, 0, False)
                back(TILES - 1, 1)
                pe.wait_ge(a_qkT, START + TILES)
                for m in range(AHEAD):
                    queries(0, m)
                for m in range(SHIFT):
                    do("micro", m, 0, False)

            run(pe, do, prologue)

    return nc


def kernel(**inputs):
    import ml_dtypes
    import numpy as np
    import concourse.bacc as bacc
    from concourse.bass_utils import run_bass_kernel_spmd

    nc = bacc.Bacc("TRN2", target_bir_lowering=False, num_devices=1)
    names = ["L0_attn_x", "L0_attn_norm_g", "L0_attn_Wq", "L0_attn_Wkv", "L0_attn_Wout", "L0_attn_out_norm_g",
             "L0_ffn_wqkv", "L0_ffn_q_scale", "L0_ffn_k_scale", "L0_ffn_wo", "L0_ffn_ln_g", "L0_ffn_ln_b",
             "L0_ffn_w1", "L0_ffn_b1", "L0_ffn_w2", "L0_ffn_b2"]
    arrays = {name: np.ascontiguousarray(inputs[name]) for name in names}
    for name in ("L0_ffn_ln_g", "L0_ffn_ln_b"):
        arrays[name] = np.ascontiguousarray(arrays[name].T)
    B, N, D = arrays["L0_attn_x"].shape
    DH, WINDOW, P = arrays["L0_ffn_q_scale"].shape[1], 64, 128
    f4 = np.float32
    half_idx = np.arange(0, DH, 2, dtype=f4)
    inv_freq = (f4(1.0) / f4(10000.0) ** (half_idx / f4(DH))).astype(f4)
    t = np.arange(N, dtype=f4)
    freqs = (t[:, None] * inv_freq[None, :]).astype(f4)
    base = ((half_idx + f4(0.4 * DH)) / f4(1.4 * DH)).astype(f4)
    scale = (base[None, :] ** ((t - N // 2) / f4(WINDOW // 2))[:, None]).astype(f4)
    cos, sin = np.cos(freqs), np.sin(freqs)
    both = lambda a, b: np.concatenate([a, b], axis=1).astype(f4)
    qs, ks = 8 * scale, 1 / scale
    arrays["rope"] = np.stack([both(cos * qs, cos * qs), both(cos * ks, cos * ks),
                               both(-sin * qs, sin * qs), both(-sin * ks, sin * ks)])
    arrays["ident"] = np.eye(P, dtype=f4)
    arrays["identh"] = np.eye(P, dtype=np.float16)
    first = np.zeros((P, P), f4)
    first[P - 1, 0] = 1
    arrays["shift"] = np.stack([np.eye(P, k=1, dtype=f4), first])
    i, j = np.arange(P)[:, None], np.arange(P)[None, :]
    low = i < WINDOW
    own = np.where(low, (j < WINDOW) & (j <= i), (j <= i) & (i - j <= WINDOW))
    prev = low & (j >= WINDOW) & (j >= i + WINDOW)
    arrays["mask"] = np.stack([np.eye(P), np.where(own, 0, -1e38), np.where(own | prev, 0, -1e38)])\
        .astype(ml_dtypes.bfloat16)
    arrays["keep"] = np.stack([np.ones(P), np.zeros(P)], axis=1).astype(f4)
    args = [nc.dram_tensor("in_" + k, v.shape, mybir.dt.from_np(v.dtype), kind="ExternalInput").ap()
            for k, v in arrays.items()]
    out = nc.dram_tensor("out", (B, N, D), mybir.dt.float32, kind="ExternalOutput").ap()
    gated_mqa_local_block(nc, *args, out)
    r = run_bass_kernel_spmd(nc, [{"in_" + k: v for k, v in arrays.items()}], core_ids=[0])
    return r.results[0]["out"]
```
